# Optimizing a Trainium2 kernel written in Bass

```python
import numpy as np
import jax
import jax.numpy as jnp

def _softmax(x, axis=-1):
    return jax.nn.softmax(x, axis=axis)

def _gelu(x):
    return jax.nn.gelu(x, approximate=True)

def _silu(x):
    return jax.nn.silu(x)

def _sigmoid(x):
    return jax.nn.sigmoid(x)

def _layernorm(x, axis=-1, eps=1e-05):
    m = jnp.mean(x, axis=axis, keepdims=True)
    v = jnp.var(x, axis=axis, keepdims=True)
    return (x - m) / jnp.sqrt(v + eps)

def _scatter_add(tgt, idx, src, axis=0):
    return tgt.at[idx].add(src)

def _segment_sum(src, seg, n):
    return jax.ops.segment_sum(src, seg, n)
kernel_name = 'mk_dlrm_tower_d1_rec_r8_ccd749'

def setup_inputs(seed: int=0):
    np.random.seed(seed)
    _w = jnp.asarray

    def _rec_inputs():
        import jax
        import jax.numpy as jnp
        _tk = jax.random.key(seed)
        dense_ctx = jax.random.normal(jax.random.fold_in(_tk, 190), (512, 16), jnp.float32)
        ids = jnp.stack([jax.random.randint(jax.random.fold_in(_tk, 200 + f), (512,), 0, v, jnp.int32) for f, v in enumerate([1250, 1250, 1000, 1000, 1000, 1000, 12500, 1250, 125000, 1000, 1250, 1250, 125000, 125000, 1000, 1250, 1250, 1250, 1000, 12500, 12500, 1000, 1250, 1000, 12500, 1250, 1250, 1000, 1000, 12500, 125000, 1000])], axis=1)
        tbl_0 = 0.05 * jax.random.normal(jax.random.fold_in(_tk, 500 + 0), (1250, 32), jnp.float32)
        tbl_1 = 0.05 * jax.random.normal(jax.random.fold_in(_tk, 500 + 1), (1250, 32), jnp.float32)
        tbl_2 = 0.05 * jax.random.normal(jax.random.fold_in(_tk, 500 + 2), (1000, 32), jnp.float32)
        tbl_3 = 0.05 * jax.random.normal(jax.random.fold_in(_tk, 500 + 3), (1000, 32), jnp.float32)
        tbl_4 = 0.05 * jax.random.normal(jax.random.fold_in(_tk, 500 + 4), (1000, 32), jnp.float32)
        tbl_5 = 0.05 * jax.random.normal(jax.random.fold_in(_tk, 500 + 5), (1000, 32), jnp.float32)
        tbl_6 = 0.05 * jax.random.normal(jax.random.fold_in(_tk, 500 + 6), (12500, 32), jnp.float32)
        tbl_7 = 0.05 * jax.random.normal(jax.random.fold_in(_tk, 500 + 7), (1250, 32), jnp.float32)
        tbl_8 = 0.05 * jax.random.normal(jax.random.fold_in(_tk, 500 + 8), (125000, 32), jnp.float32)
        tbl_9 = 0.05 * jax.random.normal(jax.random.fold_in(_tk, 500 + 9), (1000, 32), jnp.float32)
        tbl_10 = 0.05 * jax.random.normal(jax.random.fold_in(_tk, 500 + 10), (1250, 32), jnp.float32)
        tbl_11 = 0.05 * jax.random.normal(jax.random.fold_in(_tk, 500 + 11), (1250, 32), jnp.float32)
        tbl_12 = 0.05 * jax.random.normal(jax.random.fold_in(_tk, 500 + 12), (125000, 32), jnp.float32)
        tbl_13 = 0.05 * jax.random.normal(jax.random.fold_in(_tk, 500 + 13), (125000, 32), jnp.float32)
        tbl_14 = 0.05 * jax.random.normal(jax.random.fold_in(_tk, 500 + 14), (1000, 32), jnp.float32)
        tbl_15 = 0.05 * jax.random.normal(jax.random.fold_in(_tk, 500 + 15), (1250, 32), jnp.float32)
        tbl_16 = 0.05 * jax.random.normal(jax.random.fold_in(_tk, 500 + 16), (1250, 32), jnp.float32)
        tbl_17 = 0.05 * jax.random.normal(jax.random.fold_in(_tk, 500 + 17), (1250, 32), jnp.float32)
        tbl_18 = 0.05 * jax.random.normal(jax.random.fold_in(_tk, 500 + 18), (1000, 32), jnp.float32)
        tbl_19 = 0.05 * jax.random.normal(jax.random.fold_in(_tk, 500 + 19), (12500, 32), jnp.float32)
        tbl_20 = 0.05 * jax.random.normal(jax.random.fold_in(_tk, 500 + 20), (12500, 32), jnp.float32)
        tbl_21 = 0.05 * jax.random.normal(jax.random.fold_in(_tk, 500 + 21), (1000, 32), jnp.float32)
        tbl_22 = 0.05 * jax.random.normal(jax.random.fold_in(_tk, 500 + 22), (1250, 32), jnp.float32)
        tbl_23 = 0.05 * jax.random.normal(jax.random.fold_in(_tk, 500 + 23), (1000, 32), jnp.float32)
        tbl_24 = 0.05 * jax.random.normal(jax.random.fold_in(_tk, 500 + 24), (12500, 32), jnp.float32)
        tbl_25 = 0.05 * jax.random.normal(jax.random.fold_in(_tk, 500 + 25), (1250, 32), jnp.float32)
        tbl_26 = 0.05 * jax.random.normal(jax.random.fold_in(_tk, 500 + 26), (1250, 32), jnp.float32)
        tbl_27 = 0.05 * jax.random.normal(jax.random.fold_in(_tk, 500 + 27), (1000, 32), jnp.float32)
        tbl_28 = 0.05 * jax.random.normal(jax.random.fold_in(_tk, 500 + 28), (1000, 32), jnp.float32)
        tbl_29 = 0.05 * jax.random.normal(jax.random.fold_in(_tk, 500 + 29), (12500, 32), jnp.float32)
        tbl_30 = 0.05 * jax.random.normal(jax.random.fold_in(_tk, 500 + 30), (125000, 32), jnp.float32)
        tbl_31 = 0.05 * jax.random.normal(jax.random.fold_in(_tk, 500 + 31), (1000, 32), jnp.float32)
        _rk = jax.random.fold_in(_tk, 7)
        W_top1 = 0.0830455 * jax.random.normal(jax.random.fold_in(_tk, 801), (145, 512), jnp.float32)
        W_top2 = 0.0441942 * jax.random.normal(jax.random.fold_in(_tk, 802), (512, 256), jnp.float32)
        W_top3 = 0.0625 * jax.random.normal(jax.random.fold_in(_tk, 803), (256, 1), jnp.float32)
        b_top1 = jnp.zeros((512,), jnp.float32)
        b_top2 = jnp.zeros((256,), jnp.float32)
        return (dense_ctx, ids, tbl_0, tbl_1, tbl_2, tbl_3, tbl_4, tbl_5, tbl_6, tbl_7, tbl_8, tbl_9, tbl_10, tbl_11, tbl_12, tbl_13, tbl_14, tbl_15, tbl_16, tbl_17, tbl_18, tbl_19, tbl_20, tbl_21, tbl_22, tbl_23, tbl_24, tbl_25, tbl_26, tbl_27, tbl_28, tbl_29, tbl_30, tbl_31, W_top1, b_top1, W_top2, b_top2, W_top3)
    dense_ctx, ids, tbl_0, tbl_1, tbl_2, tbl_3, tbl_4, tbl_5, tbl_6, tbl_7, tbl_8, tbl_9, tbl_10, tbl_11, tbl_12, tbl_13, tbl_14, tbl_15, tbl_16, tbl_17, tbl_18, tbl_19, tbl_20, tbl_21, tbl_22, tbl_23, tbl_24, tbl_25, tbl_26, tbl_27, tbl_28, tbl_29, tbl_30, tbl_31, W_top1, b_top1, W_top2, b_top2, W_top3 = _rec_inputs()

    def _L0_rec_setup():
        import jax, jax.numpy as jnp
        import numpy as np

        def _cin(x, Ws, bs):
            B, F, D = x.shape
            h = x
            directs = []
            n_layers = len(Ws)
            for i, (W, b) in enumerate(zip(Ws, bs)):
                O = W.shape[0]
                H = h.shape[1]
                z = jnp.einsum('bhd,bmd,ohm->bod', h, x, W.reshape(O, H, F))
                z = jax.nn.relu(z + b[None, :, None])
                if i < n_layers - 1:
                    half = O // 2
                    h, direct = (z[:, :half, :], z[:, half:, :])
                else:
                    direct = z
                directs.append(direct)
            out = jnp.concatenate(directs, axis=1)
            return jnp.sum(out, axis=-1)
        key = jax.random.key(seed)
        ks = jax.random.split(key, 4)
        B, F, D = (256, 32, 32)
        x = jax.random.normal(ks[0], (B, F, D), dtype=jnp.float32)
        W0 = jax.random.normal(ks[1], (128, 32 * F), dtype=jnp.float32) * 0.05
        W1 = jax.random.normal(ks[2], (128, 64 * F), dtype=jnp.float32) * 0.05
        W2 = jax.random.normal(ks[3], (1, 64 * F), dtype=jnp.float32) * 0.05
        return {'x': x, 'W0': W0, 'b0': jnp.zeros((128,), jnp.float32), 'W1': W1, 'b1': jnp.zeros((128,), jnp.float32), 'W2': W2, 'b2': jnp.zeros((1,), jnp.float32)}
    _L0_rec_all = _L0_rec_setup()
    _L0_rec_in = {k: v for k, v in _L0_rec_all.items() if k in ('W0', 'b0', 'W1', 'b1', 'W2', 'b2')}
    del _L0_rec_all
    return {'dense_ctx': dense_ctx, 'ids': ids, 'tbl_0': tbl_0, 'tbl_1': tbl_1, 'tbl_2': tbl_2, 'tbl_3': tbl_3, 'tbl_4': tbl_4, 'tbl_5': tbl_5, 'tbl_6': tbl_6, 'tbl_7': tbl_7, 'tbl_8': tbl_8, 'tbl_9': tbl_9, 'tbl_10': tbl_10, 'tbl_11': tbl_11, 'tbl_12': tbl_12, 'tbl_13': tbl_13, 'tbl_14': tbl_14, 'tbl_15': tbl_15, 'tbl_16': tbl_16, 'tbl_17': tbl_17, 'tbl_18': tbl_18, 'tbl_19': tbl_19, 'tbl_20': tbl_20, 'tbl_21': tbl_21, 'tbl_22': tbl_22, 'tbl_23': tbl_23, 'tbl_24': tbl_24, 'tbl_25': tbl_25, 'tbl_26': tbl_26, 'tbl_27': tbl_27, 'tbl_28': tbl_28, 'tbl_29': tbl_29, 'tbl_30': tbl_30, 'tbl_31': tbl_31, 'W_top1': W_top1, 'b_top1': b_top1, 'W_top2': W_top2, 'b_top2': b_top2, 'W_top3': W_top3, 'L0_rec_W0': _L0_rec_in['W0'], 'L0_rec_b0': _L0_rec_in['b0'], 'L0_rec_W1': _L0_rec_in['W1'], 'L0_rec_b1': _L0_rec_in['b1'], 'L0_rec_W2': _L0_rec_in['W2'], 'L0_rec_b2': _L0_rec_in['b2']}

def reference(dense_ctx, ids, tbl_0, tbl_1, tbl_2, tbl_3, tbl_4, tbl_5, tbl_6, tbl_7, tbl_8, tbl_9, tbl_10, tbl_11, tbl_12, tbl_13, tbl_14, tbl_15, tbl_16, tbl_17, tbl_18, tbl_19, tbl_20, tbl_21, tbl_22, tbl_23, tbl_24, tbl_25, tbl_26, tbl_27, tbl_28, tbl_29, tbl_30, tbl_31, W_top1, b_top1, W_top2, b_top2, W_top3, L0_rec_W0, L0_rec_b0, L0_rec_W1, L0_rec_b1, L0_rec_W2, L0_rec_b2):
    import jax
    import jax.numpy as jnp

    def _L0_rec_ref(x, W0, b0, W1, b1, W2, b2):
        import jax, jax.numpy as jnp
        import numpy as np

        def _cin(x, Ws, bs):
            B, F, D = x.shape
            h = x
            directs = []
            n_layers = len(Ws)
            for i, (W, b) in enumerate(zip(Ws, bs)):
                O = W.shape[0]
                H = h.shape[1]
                z = jnp.einsum('bhd,bmd,ohm->bod', h, x, W.reshape(O, H, F))
                z = jax.nn.relu(z + b[None, :, None])
                if i < n_layers - 1:
                    half = O // 2
                    h, direct = (z[:, :half, :], z[:, half:, :])
                else:
                    direct = z
                directs.append(direct)
            out = jnp.concatenate(directs, axis=1)
            return jnp.sum(out, axis=-1)
        return _cin(x, (W0, W1, W2), (b0, b1, b2))
    e = jnp.stack([tbl_0[ids[:, 0]], tbl_1[ids[:, 1]], tbl_2[ids[:, 2]], tbl_3[ids[:, 3]], tbl_4[ids[:, 4]], tbl_5[ids[:, 5]], tbl_6[ids[:, 6]], tbl_7[ids[:, 7]], tbl_8[ids[:, 8]], tbl_9[ids[:, 9]], tbl_10[ids[:, 10]], tbl_11[ids[:, 11]], tbl_12[ids[:, 12]], tbl_13[ids[:, 13]], tbl_14[ids[:, 14]], tbl_15[ids[:, 15]], tbl_16[ids[:, 16]], tbl_17[ids[:, 17]], tbl_18[ids[:, 18]], tbl_19[ids[:, 19]], tbl_20[ids[:, 20]], tbl_21[ids[:, 21]], tbl_22[ids[:, 22]], tbl_23[ids[:, 23]], tbl_24[ids[:, 24]], tbl_25[ids[:, 25]], tbl_26[ids[:, 26]], tbl_27[ids[:, 27]], tbl_28[ids[:, 28]], tbl_29[ids[:, 29]], tbl_30[ids[:, 30]], tbl_31[ids[:, 31]]], axis=1)
    z = _L0_rec_ref(e, L0_rec_W0, L0_rec_b0, L0_rec_W1, L0_rec_b1, L0_rec_W2, L0_rec_b2)
    z = z.reshape(z.shape[0], -1)
    h = jnp.concatenate([z, dense_ctx], axis=1)
    h = jnp.maximum(h @ W_top1 + b_top1, 0.0)
    h = jnp.maximum(h @ W_top2 + b_top2, 0.0)
    y = h @ W_top3
    return y

_drawn_inputs = setup_inputs


def setup_inputs(seed=0):
    import zlib

    import numpy as np

    out = dict(_drawn_inputs(seed))
    spreads = {'b_top1': (0.0, 2.0),
     'b_top2': (0.0, 0.437),
     'L0_rec_b0': (0.0, 0.1),
     'L0_rec_b1': (0.0, 0.1)}
    factors = {'tbl_0': 8.0,
     'tbl_1': 8.0,
     'tbl_2': 8.0,
     'tbl_3': 8.0,
     'tbl_4': 8.0,
     'tbl_5': 8.0,
     'tbl_6': 8.0,
     'tbl_7': 8.0,
     'tbl_8': 8.0,
     'tbl_9': 8.0,
     'tbl_10': 8.0,
     'tbl_11': 8.0,
     'tbl_12': 8.0,
     'tbl_13': 8.0,
     'tbl_14': 8.0,
     'tbl_15': 8.0,
     'tbl_16': 8.0,
     'tbl_17': 8.0,
     'tbl_18': 8.0,
     'tbl_19': 8.0,
     'tbl_20': 8.0,
     'tbl_21': 8.0,
     'tbl_22': 8.0,
     'tbl_23': 8.0,
     'tbl_24': 8.0,
     'tbl_25': 8.0,
     'tbl_26': 8.0,
     'tbl_27': 8.0,
     'tbl_28': 8.0,
     'tbl_29': 8.0,
     'tbl_30': 8.0,
     'tbl_31': 8.0,
     'L0_rec_W0': 8.0,
     'L0_rec_W1': 3.576,
     'L0_rec_W2': 8.0,
     'dense_ctx': 3.491}
    for name, (base, spread) in spreads.items():
        noise = np.random.default_rng([zlib.crc32(name.encode()), seed]).standard_normal(out[name].shape)
        drawn = base * np.exp(spread * noise) if base else spread * noise
        out[name] = jnp.asarray(drawn.astype(out[name].dtype))
    for name, factor in factors.items():
        out[name] = (out[name] * factor).astype(out[name].dtype)
    return out
```

```python
from contextlib import ExitStack

import concourse.bass as bass
from concourse import mybir

F32 = mybir.dt.float32
I32 = mybir.dt.int32
ALU = mybir.AluOpType
ACT = mybir.ActivationFunctionType
AX = mybir.AxisListType

B, F, D = 512, 32, 32
H = 64
O = 2 * H
NDENSE = 16
U1, U2 = 512, 256

P = 128
NT = B // P
DC = 8
KC = D // DC
NCH = NT * KC
C = P * DC
HC = C // 2
Q4 = C // 4
G4 = P // F
NS = F // G4
SLO = NS // 2
RING = 4
PAIRS0 = SLO // 2
PAIRS1 = 2 * NS // 2
PAIRS = PAIRS0 + PAIRS1
XQR = 4



def build(nc, tables, ids, dense_t, w0a, w0b, w0r, w1, w2, bias_cin, b2, wt1a, wt1b, bt1, wt2, bt2, wt3,
          ident_in, ones_in, mask_in, y_out):
    scratch = nc.dram_tensor("x_fields", (NCH, 2 * F, C), F32).ap()

    with ExitStack() as ctx:
        def sb(name, shape, dt=F32):
            return ctx.enter_context(nc.sbuf_tensor(name, shape, dt))

        def ps(name, shape):
            return ctx.enter_context(nc.psum_tensor(name, shape, F32))

        def sem(name):
            return ctx.enter_context(nc.semaphore(name))

        ids_sb = sb("ids_sb", [P, F], I32)
        gathered = sb("gathered", [P, F, D])
        emb = sb("emb", [P, D, G4, F])
        x4 = sb("x4", [P, 2, C])
        xs_lo = sb("xs_lo", [P, 2, SLO, C])
        xs_hi = sb("xs_hi", [P, 2, SLO, C])
        x16 = sb("x16", [F, 2, C])
        xq = sb("xq", [P, XQR, Q4])
        hid = sb("hid", [P, 2, 2, C])
        prod = sb("prod", [P, RING, 2, C])
        prod16 = sb("prod16", [2 * F, HC])
        direct = sb("direct", [P, 2, C])
        h1 = sb("h1", [P, C])
        qprod = sb("qprod", [P, Q4])
        z2 = sb("z2", [4, KC, Q4])
        dsum = sb("dsum", [P, KC, P])
        z2sum = sb("z2sum", [4, F])
        feat = sb("feat", [P, B])
        feat_small = sb("feat_small", [4 + NDENSE, B])
        hid1 = x4[:].rearrange("p s (i b) -> p (s i) b", b=B)
        hid2 = hid[:, 0, 0, :].rearrange("p (i b) -> p i b", b=B)
        y_sb = sb("y_sb", [P, NT])
        w0_sb = sb("w0_sb", [P, SLO, O])
        w0b_sb = prod[:, RING - 1, 0, 0:SLO * O].rearrange("p (t o) -> p t o", o=O)
        w0r_sb = sb("w0r_sb", [2 * F, O])
        w1_sb = sb("w1_sb", [P, NS, 2, O])
        w2_sb = sb("w2_sb", [P, F])
        bias_sb = sb("bias_sb", [P, 2])
        b2_sb = sb("b2_sb", [4, 1])
        wt1a_sb = sb("wt1a_sb", [P, U1])
        wt1b_sb = sb("wt1b_sb", [4 + NDENSE, U1])
        bt1_sb = sb("bt1_sb", [P, U1 // P])
        wt2_sb = sb("wt2_sb", [P, U1 // P, U2])
        bt2_sb = sb("bt2_sb", [P, U2 // P])
        wt3_sb = sb("wt3_sb", [P, U2 // P])
        ident = sb("ident", [P, P])
        ones = sb("ones", [P, 4])
        mask = sb("mask", [4, 4, F])

        z0_ps = ps("z0_ps", [P, 2, HC])
        z1_ps = ps("z1_ps", [P, 2, HC])
        t_ps = ps("t_ps", [P, DC // 2, P])
        q_ps = ps("q_ps", [P, 512])
        s_ps = ps("s_ps", [P, 512])

        s_w = sem("w_loaded")
        s_ids = sem("ids_loaded")
        s_gather = sem("rows_gathered")
        s_emb = sem("emb_ready")
        s_t = sem("transposed")
        s_x4 = sem("x4_ready")
        s_store = [sem(f"x_stored{i}") for i in range(2)]
        s_lo = [sem(f"lo_loaded{i}") for i in range(2)]
        s_hi = [sem(f"hi_loaded{i}") for i in range(2)]
        s_x16 = [sem(f"x16_loaded{i}") for i in range(2)]
        s_xq = [sem(f"xq_loaded{i}") for i in range(XQR)]
        s_fold = sem("w0_folded")
        s_prod = sem("prod_ready")
        s_used = sem("prod_used")
        s_p16 = sem("prod16_ready")
        s_p16u = sem("prod16_used")
        s_hid = sem("hid_ready")
        s_z0e = sem("z0_copied")
        s_z1e = sem("z1_copied")
        s_q = sem("q_ready")
        s_qp = sem("qprod_ready")
        s_s = sem("s_ready")
        s_z2 = sem("z2_ready")
        s_dsum = sem("dsum_ready")
        s_z2s = sem("z2sum_ready")
        s_feat = sem("feat_ready")
        s_m1 = sem("tower1_ready")
        s_m1e = sem("tower1_copied")
        s_m2 = sem("tower2_ready")
        s_m2e = sem("tower2_copied")
        s_y = sem("y_ready")
        s_ye = sem("y_copied")
        s_out = sem("y_stored")
        s_apart = sem("waits_apart")

        def pairs0(g, r, i):
            return i if isinstance(g, int) and KC * g + r == 0 else PAIRS * (KC * g + r - 1) + PAIRS0 + i

        def pairs1(g, r, i):
            last = isinstance(g, int) and KC * g + r == NCH - 1
            return PAIRS * (KC * g + r) + PAIRS0 + i + (0 if last else PAIRS0)

        def ring0(g, r, i):
            return (pairs0(0, r, i) if isinstance(g, int) and g == 0 else PAIRS * (r - 1) + PAIRS0 + i) % RING

        def ring1(g, r, i):
            return (pairs1(g, r, i) if isinstance(g, int) else pairs1(0, r, i)) % RING

        def wait_apart(eng, semaphore, value):
            eng.wait_ge(semaphore, value)
            eng.sem_inc(s_apart, 1)

        block = ctx.enter_context(nc.Block())

        def stages(eng, stage):
            stage(0, 0)
            stage(0, 1)
            with eng.Fori(0, NT - 1) as g:
                for r in range(2, 2 + KC):
                    stage(g, r)
            stage(NT - 1, 2)
            stage(NT - 1, 3)

        def after(g, r):
            last = isinstance(g, int) and g == NT - 1
            return not (isinstance(g, int) and g == 0 and r == 0), not (last and r == 3), not last

        @block.gpsimd
        def _(pool):
            def gather(g, first):
                pool.dma_start(ids_sb[:], ids[bass.ds(g, 1), :, :].rearrange("t p f -> (t p) f")).then_inc(s_ids, 16)
                wait_apart(pool, s_ids, 16 * (g + 1))
                if not first:
                    wait_apart(pool, s_emb, KC * g)
                for f in range(F):
                    pool.indirect_dma_start(
                        out=gathered[:, f, :], out_offset=None, in_=tables[f],
                        in_offset=bass.IndirectOffsetOnAxis(ap=ids_sb[:, f:f + 1], axis=0),
                    ).then_inc(s_gather, 16)
                wait_apart(pool, s_gather, 16 * F * (g + 1))
                if not first:
                    wait_apart(pool, s_t, 2 * KC * g)
                for k in range(KC):
                    src = gathered[:, :, DC * k:DC * k + DC].rearrange("p f d -> p d f")
                    pool.tensor_copy(emb[:, DC * k:DC * k + DC, :, :],
                                     src.unsqueeze(2).broadcast_to([P, DC, G4, F])).then_inc(s_emb, 1)

            gather(0, True)
            with pool.Fori(1, NT) as g:
                gather(g, False)

        @block.sync
        def _(sp):
            def spread(g, k):
                c = KC * g + k
                p = k % 2
                first = isinstance(g, int)
                wait_apart(sp, s_x4, 2 * (c + 1))
                sp.dma_start(scratch[bass.ds(c, 1), :, :].rearrange("a m n -> (a m) n"),
                             x4[0:2 * F, p, :]).then_inc(s_store[p], 16)
                wait_apart(sp, s_store[p], 16 * ((KC // 2) * g + k // 2 + 1))
                src = scratch[bass.ds(c, 1), :, :].rearrange("a m n -> (a m) n")
                if not first or k >= 2:
                    wait_apart(sp, s_prod, pairs1(g, k - 2, PAIRS1 // 2))
                for q in range(G4):
                    for t in range(SLO):
                        sp.dma_start(xs_lo[F * q:F * q + F, p, t, :],
                                     src[q + G4 * t:q + G4 * t + F, :]).then_inc(s_lo[p], 16)
                if not first or k >= 2:
                    wait_apart(sp, s_p16, 2 * (c - 1))
                sp.dma_start(x16[:, p, :], src[F // 2:F // 2 + F, :]).then_inc(s_x16[p], 16)
                if not first:
                    wait_apart(sp, s_qp, c - 3)
                for j in range(4):
                    sp.dma_start(xq[F * j:F * j + F, k, :],
                                 src[0:F, Q4 * j:Q4 * j + Q4]).then_inc(s_xq[k], 16)
                if not first or k >= 2:
                    wait_apart(sp, s_prod, pairs1(g, k - 2, PAIRS1))
                for q in range(G4):
                    for t in range(SLO):
                        at = q + G4 * (SLO + t)
                        sp.dma_start(xs_hi[F * q:F * q + F, p, t, :],
                                     src[at:at + F, :]).then_inc(s_hi[p], 16)

            for k in range(KC):
                spread(0, k)
            with sp.Fori(1, NT) as g:
                for k in range(KC):
                    spread(g, k)
            sp.wait_ge(s_ye, 1)
            sp.dma_start(y_out.rearrange("(p t) o -> p (t o)", t=NT), y_sb[:]).then_inc(s_out, 16)
            sp.wait_ge(s_out, 16)

        @block.scalar
        def _(act):
            loads = [(ident[:], ident_in), (w0_sb[:], w0a), (w0b_sb, w0b), (w0r_sb[:], w0r),
                     (bias_sb[:], bias_cin), (w1_sb[:], w1), (w2_sb[H:P, :], w2), (b2_sb[:], b2),
                     (ones[:], ones_in), (mask[:], mask_in), (feat_small[4:4 + NDENSE, :], dense_t),
                     (wt1a_sb[:], wt1a), (wt1b_sb[:], wt1b), (bt1_sb[:], bt1), (wt2_sb[:], wt2),
                     (bt2_sb[:], bt2), (wt3_sb[:], wt3)]
            for dst, src in loads:
                act.dma_start(dst, src).then_inc(s_w, 16)

            def copy_x(g, r, half):
                c = KC * g + r
                act.wait_ge(s_t, 2 * c + half + 1)
                if half == 0 and not (isinstance(g, int) and g == 0 and r < 2):
                    act.wait_ge(s_p16, 2 * (c - 1))
                    act.wait_ge(s_store[r % 2], 16 * ((KC // 2) * g + r // 2))
                dst = x4[:, r % 2, :].rearrange("p (b d) -> p b d", d=DC)
                nc.scalar.activation(dst[:, :, half * DC // 2:(half + 1) * DC // 2],
                                     t_ps[:].rearrange("p d b -> p b d"), ACT.Copy).then_inc(s_x4, 1)

            def copy_z0(g, r):
                c = KC * g + r
                s = r % 2
                act.wait_ge(s_p16u, c + 1)
                if not (isinstance(g, int) and g == 0 and r < 2):
                    act.wait_ge(s_prod, pairs1(g, r - 2, PAIRS1))
                z = z0_ps[:].rearrange("p h n -> p (h n)")

                def relu(out, lo, n):
                    return nc.scalar.activation(out, z[lo:lo + n, :], ACT.Relu, bias=bias_sb[lo:lo + n, 0:1])
                relu(hid[0:H, s, 0, :], 0, H)
                relu(hid[H:P, s, 0, :], 0, H)
                for q in range(G4):
                    last = relu(hid[F * q:F * q + F, s, 1, :], F * ((q + 1) % 2), F)
                last.then_inc(s_hid, 1)
                if not (isinstance(g, int) and g == 0 and r < 2):
                    act.wait_ge(s_dsum, c - 1)
                relu(direct[H:P, s, :], H, H).then_inc(s_z0e, 1)

            def copy_z1(g, r):
                c = KC * g + r
                act.wait_ge(s_used, pairs1(g, r, PAIRS1))
                z = z1_ps[:].rearrange("p h n -> p (h n)")
                nc.scalar.activation(direct[0:H, r % 2, :], z[0:H, :], ACT.Relu, bias=bias_sb[0:H, 1:2])
                if after(g, r)[0]:
                    act.wait_ge(s_q, c)
                nc.scalar.activation(h1[H:P, :], z[H:P, :], ACT.Relu, bias=bias_sb[H:P, 1:2]).then_inc(s_z1e, 1)

            def copy_z2(g, r):
                c = KC * g + r
                act.wait_ge(s_s, c + 1)
                if r % KC == 0 and not (isinstance(g, int) and g == 0 and r == 0):
                    act.wait_ge(s_z2s, g + r // KC)
                nc.scalar.activation(z2[:, r % KC, :], s_ps[0:4, 0:Q4], ACT.Relu,
                                     bias=b2_sb[:, 0:1]).then_inc(s_z2, 1)

            def stage(g, r):
                before, next1, next2 = after(g, r)
                if next2:
                    copy_x(g, r + 2, 0)
                if next1:
                    copy_z0(g, r + 1)
                if next2:
                    copy_x(g, r + 2, 1)
                if before:
                    copy_z2(g, r - 1)
                copy_z1(g, r)

            act.wait_ge(s_w, 16 * len(loads))
            for r in range(2):
                copy_x(0, r, 0)
                copy_x(0, r, 1)
            copy_z0(0, 0)
            stages(act, stage)
            copy_z2(NT - 1, KC - 1)

            for i in range(U1 // P):
                act.wait_ge(s_m1, i + 1)
                bank = (z0_ps, z1_ps)[i // 2][:, i % 2, :]
                nc.scalar.activation(hid1[:, i, :], bank, ACT.Relu, bias=bt1_sb[:, i:i + 1]).then_inc(s_m1e, 1)
            for i in range(U2 // P):
                act.wait_ge(s_m2, i + 1)
                bank = (t_ps[:].rearrange("p d b -> p (d b)"), q_ps[:])[i]
                nc.scalar.activation(hid2[:, i, :], bank, ACT.Relu, bias=bt2_sb[:, i:i + 1]).then_inc(s_m2e, 1)
            act.wait_ge(s_y, 1)
            nc.scalar.activation(y_sb[:], s_ps[:, 0:NT], ACT.Copy).then_inc(s_ye, 1)

        @block.vector
        def _(dve):
            dve.wait_ge(s_w, 16 * 17)
            for at in ((slice(F, 2 * F), slice(0, 1)), (slice(2 * F, P), slice(0, 1)), (slice(0, P), slice(1, SLO))):
                dve.tensor_tensor(w0_sb[at[0], at[1], :], w0_sb[at[0], at[1], :], w0b_sb[at[0], at[1], :],
                                  ALU.add).then_inc(s_fold, 1)

            def pair(n, to, x0, x1):
                if not isinstance(n, int) or n >= RING:
                    dve.wait_ge(s_used, n - RING + 1)
                dve.tensor_tensor(prod[:, to, :, :], x0.unsqueeze(1).broadcast_to([P, 2, C]), x1,
                                  ALU.mult).then_inc(s_prod, 1)

            def layer0(g, r):
                c = KC * g + r
                s = r % 2
                dve.wait_ge(s_x4, 2 * (c + 1))
                dve.wait_ge(s_lo[s], 16 * G4 * SLO * ((KC // 2) * g + r // 2 + 1))
                for i in range(PAIRS0):
                    pair(pairs0(g, r, i), ring0(g, r, i), x4[:, s, :], xs_lo[:, s, 2 * i:2 * i + 2, :])
                dve.wait_ge(s_x16[s], 16 * ((KC // 2) * g + r // 2 + 1))
                if not (isinstance(g, int) and g == 0 and r == 0):
                    dve.wait_ge(s_p16u, c)
                for j in range(2):
                    last = dve.tensor_tensor(prod16[F * j:F * j + F, :], x4[0:F, s, HC * j:HC * j + HC],
                                             x16[:, s, HC * j:HC * j + HC], ALU.mult)
                    last.then_inc(s_p16, 1)

            def layer1(g, r, i):
                c = KC * g + r
                s = r % 2
                t = 2 * (i // 2)
                half = ((KC // 2) * g + r // 2 + 1)
                if i == 0:
                    dve.wait_ge(s_hid, c + 1)
                if i == PAIRS1 // 2:
                    dve.wait_ge(s_hi[s], 16 * G4 * SLO * half)
                xs = xs_lo[:, s, t:t + 2, :] if t < SLO else xs_hi[:, s, t - SLO:t - SLO + 2, :]
                pair(pairs1(g, r, i), ring1(g, r, i), hid[:, s, i % 2, :], xs)

            def sum_direct(g, r):
                c = KC * g + r
                dve.wait_ge(s_z1e, c + 1)
                k = r % KC
                dve.tensor_reduce(dsum[:, k, :], direct[:, r % 2, :].rearrange("p (b d) -> p b d", d=DC),
                                  AX.X, ALU.add).then_inc(s_dsum, 1)
                if k == KC - 1:
                    dve.wait_ge(s_dsum, c + 1)
                    gb = g + r // KC
                    dve.tensor_reduce(feat[:, bass.ts(gb, P)], dsum[:].rearrange("p k b -> p b k"),
                                      AX.X, ALU.add).then_inc(s_feat, 1)

            def layer2(g, r):
                c = KC * g + r
                dve.wait_ge(s_q, c + 1)
                dve.wait_ge(s_xq[r % KC], 64 * (g + r // KC + 1))
                if not (isinstance(g, int) and g == 0 and r == 0):
                    dve.wait_ge(s_s, c)
                dve.tensor_tensor(qprod[:], q_ps[:, 0:Q4], xq[:, r % KC, :], ALU.mult).then_inc(s_qp, 1)

            def sum_z2(g, r):
                gb = g + r // KC
                dve.wait_ge(s_z2, KC * (gb + 1))
                dve.tensor_reduce(z2sum[:], z2[:].rearrange("p k (b d) -> p b k d", d=DC),
                                  AX.XY, ALU.add).then_inc(s_z2s, 1)
                dve.wait_ge(s_z2s, gb + 1)
                dve.tensor_tensor(feat_small[0:4, bass.ts(gb, P)].rearrange("p (j b) -> p j b", j=4),
                                  z2sum[:].unsqueeze(1).broadcast_to([4, 4, F]), mask[:],
                                  ALU.mult).then_inc(s_feat, 1)

            def stage(g, r):
                before, next1, _ = after(g, r)
                if next1:
                    layer0(g, r + 1)
                for i in range(PAIRS1):
                    layer1(g, r, i)
                    if i == 3 and before:
                        sum_direct(g, r - 1)
                    if i == 2 and before and (r - 2) % KC == KC - 1 and not (isinstance(g, int) and g == 0):
                        sum_z2(g, r - 2)
                    if i == 5 and before:
                        layer2(g, r - 1)

            layer0(0, 0)
            stages(dve, stage)
            sum_direct(NT - 1, KC - 1)
            layer2(NT - 1, KC - 1)
            sum_z2(NT - 1, KC - 1)

        @block.tensor
        def _(pe):
            def transposes(g, r, half):
                c = KC * g + r
                pe.wait_ge(s_emb, c + 1)
                if half or not (isinstance(g, int) and g == 0 and r == 0):
                    pe.wait_ge(s_x4, 2 * c + half)
                for i in range(DC // 2):
                    d = DC * (r % KC) + half * DC // 2 + i
                    last = pe.transpose(t_ps[:, i, :], emb[:, d, :, :].rearrange("p q f -> p (q f)"),
                                        ident[:])
                last.then_inc(s_t, 1)

            def matmuls(n, at, out, weights, start, stop):
                pe.wait_ge(s_prod, n + 1)
                for j in range(2):
                    for half in range(2):
                        last = pe.matmul(out[:, half, :], weights[j],
                                         prod[:, at, j, HC * half:HC * half + HC],
                                         start=start and j == 0, stop=stop and j == 1)
                last.then_inc(s_used, 1)
                return last

            def layer0(g, r):
                c = KC * g + r
                if not (isinstance(g, int) and g == 0 and r == 0):
                    pe.wait_ge(s_z0e, c)
                for i in range(PAIRS0):
                    matmuls(pairs0(g, r, i), ring0(g, r, i), z0_ps, [w0_sb[:, 2 * i + j, :] for j in range(2)], i == 0, False)
                pe.wait_ge(s_p16, 2 * (c + 1))
                for half in range(2):
                    rows = slice(F * half, F * half + F)
                    last = pe.matmul(z0_ps[:, half, :], w0r_sb[rows, :], prod16[rows, :],
                                     start=False, stop=True)
                last.then_inc(s_p16u, 1)

            def layer2_q(g, r):
                c = KC * g + r
                pe.wait_ge(s_z1e, c + 1)
                if not (isinstance(g, int) and g == 0 and r == 0):
                    wait_apart(pe, s_qp, c)
                for j in range(4):
                    last = pe.matmul(q_ps[F * j:F * j + F, 0:Q4], w2_sb[H:P, :], h1[H:P, Q4 * j:Q4 * j + Q4],
                                     start=True, stop=True)
                last.then_inc(s_q, 1)

            def layer2_sum(g, r):
                c = KC * g + r
                pe.wait_ge(s_qp, c + 1)
                if not (isinstance(g, int) and g == 0 and r == 0):
                    pe.wait_ge(s_z2, c)
                pe.matmul(s_ps[0:4, 0:Q4], ones[:], qprod[:], start=True, stop=True).then_inc(s_s, 1)

            def stage(g, r):
                before, next1, next2 = after(g, r)
                if next2:
                    transposes(g, r + 2, 0)
                if next1:
                    layer0(g, r + 1)
                if next2:
                    transposes(g, r + 2, 1)
                c = KC * g + r
                if before:
                    pe.wait_ge(s_z1e, c)
                for i in range(PAIRS1):
                    t = 2 * (i // 2)
                    matmuls(pairs1(g, r, i), ring1(g, r, i), z1_ps, [w1_sb[:, t + j, i % 2, :] for j in range(2)],
                                   i == 0, i == PAIRS1 - 1)
                    if i == 2 and before:
                        layer2_q(g, r - 1)
                    if i == 6 and before:
                        layer2_sum(g, r - 1)

            pe.wait_ge(s_w, 16 * 17)
            pe.wait_ge(s_fold, 3)
            for r in range(2):
                transposes(0, r, 0)
                transposes(0, r, 1)
            layer0(0, 0)
            stages(pe, stage)
            layer2_q(NT - 1, KC - 1)
            layer2_sum(NT - 1, KC - 1)

            pe.wait_ge(s_feat, 2 * NT)
            pe.wait_ge(s_z0e, NCH)
            for i in range(U1 // P):
                bank = (z0_ps, z1_ps)[i // 2][:, i % 2, :]
                pe.matmul(bank, wt1a_sb[:, P * i:P * i + P], feat[:], start=True, stop=False)
                pe.matmul(bank, wt1b_sb[:, P * i:P * i + P], feat_small[:], start=False, stop=True).then_inc(s_m1, 1)
            for i in range(U2 // P):
                bank = (t_ps[:].rearrange("p d b -> p (d b)"), q_ps[:])[i]
                for k in range(U1 // P):
                    if i == 0:
                        pe.wait_ge(s_m1e, k + 1)
                    last = pe.matmul(bank, wt2_sb[:, k, P * i:P * i + P], hid1[:, k, :],
                                     start=(k == 0), stop=(k == U1 // P - 1))
                last.then_inc(s_m2, 1)
            pe.wait_ge(s_m2e, U2 // P)
            for t in range(NT):
                for k in range(U2 // P):
                    last = pe.matmul(s_ps[:, t:t + 1], hid2[:, k, P * t:P * t + P], wt3_sb[:, k:k + 1],
                                     start=(k == 0), stop=(k == U2 // P - 1))
            last.then_inc(s_y, 1)


def kernel(**inputs):
    import numpy as np
    import concourse.bacc as bacc
    from concourse.bass_utils import run_bass_kernel_spmd

    a = {k: np.asarray(v) for k, v in inputs.items()}
    l = np.arange(F)
    q = np.arange(G4)[:, None]
    w0 = a["L0_rec_W0"].reshape(O, F, F)
    m = (l + q + G4 * np.arange(NS)[:, None, None]) % F
    mo = m[:SLO].transpose(1, 2, 0)
    ll = np.broadcast_to(l[None, :, None], mo.shape)
    w0a = w0[:, ll, mo].transpose(1, 2, 3, 0).reshape(P, SLO, O)
    w0b = w0[:, mo, ll].transpose(1, 2, 3, 0).reshape(P, SLO, O)
    w0r = w0[:, l, (l + F // 2) % F].T
    w1 = a["L0_rec_W1"].reshape(O, H, F)
    order = np.r_[H:O, 0:H]
    mm = np.broadcast_to(m.transpose(1, 2, 0)[..., None], (G4, F, NS, 2))
    hh = F * ((q[:, :, None, None] + np.arange(2)) % 2) + l[None, :, None, None]
    w1t = w1[order][:, np.broadcast_to(hh, mm.shape), mm].transpose(1, 2, 3, 4, 0).reshape(P, NS, 2, O)
    wt1 = a["W_top1"]
    arrays = {
        "ids": a["ids"].reshape(P, NT, F).transpose(1, 0, 2),
        "dense_t": a["dense_ctx"].reshape(P, NT, NDENSE).transpose(2, 1, 0).reshape(NDENSE, B),
        "w0a": w0a, "w0b": w0b, "w0r": np.concatenate([w0r, w0r]), "w1": w1t,
        "w2": a["L0_rec_W2"].reshape(H, F),
        "bias_cin": np.stack([a["L0_rec_b0"], a["L0_rec_b1"][order]], axis=1),
        "b2": np.repeat(a["L0_rec_b2"].reshape(1, 1), 4, axis=0),
        "wt1a": wt1[order], "wt1b": np.concatenate([np.repeat(wt1[O:O + 1], 4, axis=0), wt1[O + 1:]]),
        "bt1": a["b_top1"].reshape(U1 // P, P).T,
        "wt2": a["W_top2"].reshape(U1 // P, P, U2).transpose(1, 0, 2),
        "bt2": a["b_top2"].reshape(U2 // P, P).T, "wt3": a["W_top3"].reshape(U2 // P, P).T,
        "ident": np.eye(P, dtype=np.float32),
        "ones": np.repeat(np.eye(4, dtype=np.float32), F, axis=0),
        "mask": np.repeat(np.eye(4, dtype=np.float32), F, axis=1).reshape(4, 4, F),
    }
    arrays = {k: np.ascontiguousarray(v) for k, v in arrays.items()}
    tables = {f"tbl_{f}": a[f"tbl_{f}"] for f in range(F)}

    nc = bacc.Bacc("TRN2", target_bir_lowering=False, num_devices=1)

    def dram(name, x):
        return nc.dram_tensor(f"in_{name}", x.shape, mybir.dt.from_np(x.dtype), kind="ExternalInput").ap()
    tabs = [dram(k, v) for k, v in tables.items()]
    args = [dram(k, v) for k, v in arrays.items()]
    y = nc.dram_tensor("out_y", (B, 1), F32, kind="ExternalOutput").ap()
    build(nc, tabs, *args, y)
    feeds = {f"in_{k}": v for k, v in {**tables, **arrays}.items()}
    r = run_bass_kernel_spmd(nc, [feeds], core_ids=[0])
    return r.results[0]["out_y"]
```

```python
from contextlib import ExitStack

import concourse.bass as bass
from concourse import mybir

F32 = mybir.dt.float32
F32R = mybir.dt.float32r
I32 = mybir.dt.int32
ALU = mybir.AluOpType
ACT = mybir.ActivationFunctionType
AX = mybir.AxisListType

B, F, D = 512, 32, 32
H = 64
O = 2 * H
NDENSE = 16
U1, U2 = 512, 256

P = 128
NT = B // P
DC = 8
KC = D // DC
NCH = NT * KC
C = P * DC
HC = C // 2
Q4 = C // 4
G4 = P // F
NS = F // G4
SLO = NS // 2
RING = 2
SRING = 2
PAIRS0 = SLO // 2
PAIRS1 = NS // 2
PAIRS = PAIRS0 + PAIRS1
XQR = 4



def build(nc, tables, ids, dense_t, w0a, w0b, w0r, w1, w2, bias_cin, b2, wt1a, wt1b, bt1, wt2, bt2, wt3,
          ident_in, ones_in, mask_in, y_out):
    scratch = nc.dram_tensor("x_fields", (NCH, 2 * F, C), F32).ap()

    with ExitStack() as ctx:
        def sb(name, shape, dt=F32):
            return ctx.enter_context(nc.sbuf_tensor(name, shape, dt))

        def ps(name, shape):
            return ctx.enter_context(nc.psum_tensor(name, shape, F32))

        def sem(name):
            return ctx.enter_context(nc.semaphore(name))

        ids_sb = sb("ids_sb", [P, F], I32)
        gathered = sb("gathered", [P, F, D])
        emb = sb("emb", [P, 2, DC, G4, F])
        x4 = sb("x4", [P, 2, C])
        xs_lo = sb("xs_lo", [P, 2, SLO, C])
        xs_hi = sb("xs_hi", [P, SLO, C])
        x16 = sb("x16", [F, 2, C])
        xq = sb("xq", [P, XQR, Q4])
        hid = sb("hid", [P, 2, 2, C])
        prod = sb("prod", [P, RING, 2, C])
        raw = sb("raw", [P, 2, C])
        part_hi = sb("part_hi", [P, SRING, 2, C], F32R)
        part_lo = sb("part_lo", [P, SRING, 2, C], F32R)
        prod16 = sb("prod16", [2 * F, HC])
        direct = sb("direct", [P, 2, C])
        h1 = sb("h1", [P, C])
        qprod = sb("qprod", [P, Q4])
        z2 = sb("z2", [4, KC, Q4])
        dsum = sb("dsum", [P, KC, P])
        z2sum = sb("z2sum", [4, F])
        feat = sb("feat", [P, B])
        feat_small = sb("feat_small", [4 + NDENSE, B])
        hid1 = x4[:].rearrange("p s (i b) -> p (s i) b", b=B)
        hid2 = hid[:, 0, 0, :].rearrange("p (i b) -> p i b", b=B)
        y_sb = sb("y_sb", [P, NT])
        w0_sb = sb("w0_sb", [P, SLO, O])
        w0b_sb = raw[:, 0, 0:SLO * O].rearrange("p (t o) -> p t o", o=O)
        w0r_sb = sb("w0r_sb", [2 * F, O])
        w1_sb = sb("w1_sb", [P, NS, O])
        w1_hi = sb("w1_hi", [P, NS, O], F32R)
        w1_lo = sb("w1_lo", [P, NS, O], F32R)
        w1b_sb = hid[:, 0, 0, :].rearrange("p (t o) -> p t o", o=O)
        w2_sb = sb("w2_sb", [P, F])
        bias_sb = sb("bias_sb", [P, 2])
        b2_sb = sb("b2_sb", [4, 1])
        wt1a_sb = sb("wt1a_sb", [P, U1])
        wt1b_sb = sb("wt1b_sb", [4 + NDENSE, U1])
        bt1_sb = sb("bt1_sb", [P, U1 // P])
        wt2_sb = sb("wt2_sb", [P, U1 // P, U2])
        bt2_sb = sb("bt2_sb", [P, U2 // P])
        wt3_sb = sb("wt3_sb", [P, U2 // P])
        ident = sb("ident", [P, P])
        ones = sb("ones", [P, 4])
        mask = sb("mask", [4, 4, F])

        z0_ps = ps("z0_ps", [P, 2, HC])
        z1_ps = ps("z1_ps", [P, 2, HC])
        t_ps = ps("t_ps", [P, DC // 2, P])
        q_ps = ps("q_ps", [P, 512])
        s_ps = ps("s_ps", [P, 512])

        s_w = sem("w_loaded")
        s_ids = sem("ids_loaded")
        s_gather = sem("rows_gathered")
        s_emb = sem("emb_ready")
        s_t = sem("transposed")
        s_x4 = sem("x4_ready")
        s_store = [sem(f"x_stored{i}") for i in range(2)]
        s_lo = [sem(f"lo_loaded{i}") for i in range(2)]
        s_hi = sem("hi_loaded")
        s_x16 = [sem(f"x16_loaded{i}") for i in range(2)]
        s_xq = [sem(f"xq_loaded{i}") for i in range(XQR)]
        s_fold = sem("w0_folded")
        s_prod = sem("prod_ready")
        s_used = sem("prod_used")
        s_raw = sem("raw_ready")
        s_part_hi = sem("part_hi_ready")
        s_part_lo = sem("part_lo_ready")
        s_parts_used = sem("parts_used")
        s_p16 = sem("prod16_ready")
        s_p16u = sem("prod16_used")
        s_hid = sem("hid_ready")
        s_z0e = sem("z0_copied")
        s_z1e = sem("z1_copied")
        s_q = sem("q_ready")
        s_qp = sem("qprod_ready")
        s_s = sem("s_ready")
        s_z2 = sem("z2_ready")
        s_dsum = sem("dsum_ready")
        s_z2s = sem("z2sum_ready")
        s_feat = sem("feat_ready")
        s_m1 = sem("tower1_ready")
        s_m1e = sem("tower1_copied")
        s_m2 = sem("tower2_ready")
        s_m2e = sem("tower2_copied")
        s_y = sem("y_ready")
        s_ye = sem("y_copied")
        s_out = sem("y_stored")
        s_table = sem("table_loaded")
        s_apart = sem("waits_apart")

        def pairs0(g, r, i):
            return i if isinstance(g, int) and KC * g + r == 0 else PAIRS * (KC * g + r - 1) + PAIRS0 + i

        def pairs1(g, r, i):
            last = isinstance(g, int) and KC * g + r == NCH - 1
            return PAIRS * (KC * g + r) + PAIRS0 + i + (0 if last else PAIRS0)

        def ring0(g, r, i):
            return (pairs0(0, r, i) if isinstance(g, int) and g == 0 else PAIRS * (r - 1) + PAIRS0 + i) % RING

        def ring1(g, r, i):
            return (pairs1(g, r, i) if isinstance(g, int) else pairs1(0, r, i)) % RING

        TB = [(0, B - P), (B - P, B)]

        def bank1(i):
            return (z0_ps, z1_ps)[i // 2][:, i % 2, :]

        def bank2(i):
            return (t_ps[:].rearrange("p d b -> p (d b)"), q_ps[:])[i]

        def reorder(eng, k):
            src = gathered[:, :, DC * k:DC * k + DC].rearrange("p f d -> p d f")
            eng.tensor_copy(emb[:, k % 2, :, :, :],
                            src.unsqueeze(2).broadcast_to([P, DC, G4, F])).then_inc(s_emb, 1)

        def t_bank(g, r, half):
            first = isinstance(g, int) and g == 0 and r < 2
            return q_ps[:].rearrange("p (d b) -> p d b", b=P) if first and half else t_ps[:]

        def wait_apart(eng, semaphore, value):
            eng.wait_ge(semaphore, value)
            eng.sem_inc(s_apart, 1)

        block = ctx.enter_context(nc.Block())

        def stages(eng, stage):
            stage(0, 0)
            stage(0, 1)
            with eng.Fori(0, NT - 1) as g:
                for r in range(2, 2 + KC):
                    stage(g, r)
            stage(NT - 1, 2)
            stage(NT - 1, 3)

        def after(g, r):
            last = isinstance(g, int) and g == NT - 1
            return not (isinstance(g, int) and g == 0 and r == 0), not (last and r == 3), not last

        @block.gpsimd
        def _(pool):
            def gather(g, first):
                pool.dma_start(ids_sb[:], ids[bass.ds(g, 1), :, :].rearrange("t p f -> (t p) f")).then_inc(s_ids, 16)
                wait_apart(pool, s_ids, 16 * (g + 1))
                if not first:
                    wait_apart(pool, s_emb, KC * g)
                for f in range(F):
                    pool.indirect_dma_start(
                        out=gathered[:, f, :], out_offset=None, in_=tables[f],
                        in_offset=bass.IndirectOffsetOnAxis(ap=ids_sb[:, f:f + 1], axis=0),
                    ).then_inc(s_gather, 16)
                wait_apart(pool, s_gather, 16 * F * (g + 1))
                if first:
                    wait_apart(pool, s_emb, 2)
                for k in range(2 if first else 0, KC):
                    wait_apart(pool, s_t, 2 * (KC * g + k - 1))
                    reorder(pool, k)

            gather(0, True)
            with pool.Fori(1, NT) as g:
                gather(g, False)

        @block.sync
        def _(sp):
            def shifted(c, at, tiles):
                row = scratch[bass.ds(c, 1), at:at + 1, 0:1]
                return bass.AP(row.tensor, row.offset, [[C, F], [G4 * C, tiles], [1, C]],
                               runtime_checks=row.runtime_checks)

            def spread(g, k):
                c = KC * g + k
                p = k % 2
                first = isinstance(g, int)
                wait_apart(sp, s_x4, 2 * (c + 1))
                rows = scratch[bass.ds(c, 1), :, :].rearrange("a m n -> (a m) n")
                sp.dma_start(rows, x4[0:2 * F, p, :]).then_inc(s_store[p], 16)
                wait_apart(sp, s_store[p], 16 * ((KC // 2) * g + k // 2 + 1))
                if not first or k >= 2:
                    wait_apart(sp, s_prod, pairs1(g, k - 2, PAIRS1 // 2))
                for q in range(G4):
                    sp.dma_start(xs_lo[F * q:F * q + F, p, :, :], shifted(c, q, SLO)).then_inc(s_lo[p], 16)
                if not first or k >= 2:
                    wait_apart(sp, s_p16, 2 * (c - 1))
                sp.dma_start(x16[:, p, :], rows[F // 2:F // 2 + F, :]).then_inc(s_x16[p], 16)
                if first and k == 0:
                    return
                if first and k == 1:
                    spread_hi(0, 0)
                    spread_q(0, 0)
                spread_q(g, k)
                if not first or k >= 2:
                    spread_hi(g, k - 1)

            def spread_q(g, k):
                c = KC * g + k
                rows = scratch[bass.ds(c, 1), :, :].rearrange("a m n -> (a m) n")
                if not isinstance(g, int):
                    wait_apart(sp, s_qp, c - 3)
                for j in range(4):
                    sp.dma_start(xq[F * j:F * j + F, k, :], rows[0:F, Q4 * j:Q4 * j + Q4]).then_inc(s_xq[k], 16)

            def spread_hi(g, r):
                c = KC * g + r
                if not isinstance(g, int) or c > 0:
                    wait_apart(sp, s_prod, pairs1(g, r - 1, PAIRS1))
                for q in range(G4):
                    sp.dma_start(xs_hi[F * q:F * q + F, :, :], shifted(c, G4 * SLO + q, SLO)).then_inc(s_hi, 16)

            for k in range(KC):
                spread(0, k)
            with sp.Fori(1, NT) as g:
                for k in range(KC):
                    spread(g, k)
            spread_hi(NT - 1, KC - 1)
            sp.wait_ge(s_ye, 1)
            sp.dma_start(y_out.rearrange("(p t) o -> p (t o)", t=NT), y_sb[:]).then_inc(s_out, 16)
            sp.wait_ge(s_out, 16)

        @block.scalar
        def _(act):
            loads = [(ident[:], ident_in), (w0_sb[:], w0a), (w0b_sb, w0b), (w0r_sb[:], w0r),
                     (bias_sb[:], bias_cin), (w1_sb[:], w1[:, 0, :, :]), (w1b_sb, w1[:, 1, :, :]), (w2_sb[H:P, :], w2), (b2_sb[:], b2),
                     (ones[:], ones_in), (mask[:], mask_in), (feat_small[4:4 + NDENSE, :], dense_t),
                     (wt1a_sb[:], wt1a), (wt1b_sb[:], wt1b), (bt1_sb[:], bt1), (wt2_sb[:], wt2),
                     (bt2_sb[:], bt2), (wt3_sb[:], wt3)]
            for dst, src in loads:
                act.dma_start(dst, src).then_inc(s_w, 16)

            def copy_x(g, r, half):
                c = KC * g + r
                act.wait_ge(s_t, 2 * c + half + 1)
                if half == 0 and not (isinstance(g, int) and g == 0 and r < 2):
                    act.wait_ge(s_p16, 2 * (c - 1))
                    act.wait_ge(s_store[r % 2], 16 * ((KC // 2) * g + r // 2))
                dst = x4[:, r % 2, :].rearrange("p (b d) -> p b d", d=DC)
                nc.scalar.activation(dst[:, :, half * DC // 2:(half + 1) * DC // 2],
                                     t_bank(g, r, half).rearrange("p d b -> p b d"), ACT.Copy).then_inc(s_x4, 1)

            def round_part(g, r, i):
                n = PAIRS1 * (KC * g + r) + i
                act.wait_ge(s_raw, n + 1)
                if not isinstance(n, int) or n >= SRING:
                    act.wait_ge(s_parts_used, n - SRING + 1)
                nc.scalar.activation(part_hi[:, i % SRING, :, :], raw[:], ACT.Copy).then_inc(s_part_hi, 1)

            def copy_z0(g, r, rounds):
                c = KC * g + r
                s = r % 2
                act.wait_ge(s_p16u, c + 1)
                if not (isinstance(g, int) and g == 0 and r < 2):
                    act.wait_ge(s_prod, pairs1(g, r - 2, PAIRS1))
                z = z0_ps[:].rearrange("p h n -> p (h n)")

                def relu(out, lo, n):
                    return nc.scalar.activation(out, z[lo:lo + n, :], ACT.Relu, bias=bias_sb[lo:lo + n, 0:1])
                relu(hid[0:H, s, 0, :], 0, H)
                relu(hid[H:P, s, 0, :], 0, H)
                if rounds:
                    round_part(g, r - 1, 1)
                for q in range(G4):
                    last = relu(hid[F * q:F * q + F, s, 1, :], F * ((q + 1) % 2), F)
                last.then_inc(s_hid, 1)
                if not (isinstance(g, int) and g == 0 and r < 2):
                    act.wait_ge(s_dsum, c - 1)
                relu(direct[H:P, s, :], H, H).then_inc(s_z0e, 1)

            def copy_z1(g, r):
                c = KC * g + r
                act.wait_ge(s_parts_used, PAIRS1 * (c + 1))
                z = z1_ps[:].rearrange("p h n -> p (h n)")
                nc.scalar.activation(direct[0:H, r % 2, :], z[0:H, :], ACT.Relu, bias=bias_sb[0:H, 1:2])
                if after(g, r)[0]:
                    act.wait_ge(s_q, c)
                nc.scalar.activation(h1[H:P, :], z[H:P, :], ACT.Relu, bias=bias_sb[H:P, 1:2]).then_inc(s_z1e, 1)

            def copy_z2(g, r):
                c = KC * g + r
                act.wait_ge(s_s, c + 1)
                if r % KC == 0 and not (isinstance(g, int) and g == 0 and r == 0):
                    act.wait_ge(s_z2s, g + r // KC)
                nc.scalar.activation(z2[:, r % KC, :], s_ps[0:4, 0:Q4], ACT.Relu,
                                     bias=b2_sb[:, 0:1]).then_inc(s_z2, 1)

            def stage(g, r):
                before, next1, next2 = after(g, r)
                if next1:
                    round_part(g, r, 0)
                if next2:
                    copy_x(g, r + 2, 0)
                if next1:
                    copy_z0(g, r + 1, True)
                else:
                    round_part(g, r, 1)
                if next2:
                    copy_x(g, r + 2, 1)
                for i in range(2, PAIRS1):
                    round_part(g, r, i)
                if before:
                    copy_z2(g, r - 1)
                if next1 and not next2:
                    round_part(g, r + 1, 0)
                copy_z1(g, r)

            act.wait_ge(s_w, 16 * len(loads))
            nc.scalar.activation(y_sb[:, 0:1], bias_sb[:, 0:1], ACT.Relu).then_inc(s_table, 1)
            for r in range(2):
                copy_x(0, r, 0)
                copy_x(0, r, 1)
            copy_z0(0, 0, False)
            stages(act, stage)

            def copy_tower(n, src, dst, b, width, bias, ready, copied):
                for i in range(width // P):
                    act.wait_ge(ready, width // P * n + i + 1)
                    nc.scalar.activation(dst[:, i, b[0]:b[1]], src(i)[:, b[0]:b[1]], ACT.Relu,
                                         bias=bias[:, i:i + 1]).then_inc(copied, 1)

            copy_tower(0, bank1, hid1, TB[0], U1, bt1_sb, s_m1, s_m1e)
            copy_z2(NT - 1, KC - 1)
            copy_tower(0, bank2, hid2, TB[0], U2, bt2_sb, s_m2, s_m2e)
            copy_tower(1, bank1, hid1, TB[1], U1, bt1_sb, s_m1, s_m1e)
            copy_tower(1, bank2, hid2, TB[1], U2, bt2_sb, s_m2, s_m2e)
            act.wait_ge(s_y, 1)
            nc.scalar.activation(y_sb[:], s_ps[:, 0:NT], ACT.Copy).then_inc(s_ye, 1)

        @block.vector
        def _(dve):
            dve.wait_ge(s_w, 16 * 18)
            for at in ((slice(F, 2 * F), slice(0, 1)), (slice(2 * F, P), slice(0, 1)), (slice(0, P), slice(1, SLO))):
                dve.tensor_tensor(w0_sb[at[0], at[1], :], w0_sb[at[0], at[1], :], w0b_sb[at[0], at[1], :],
                                  ALU.add).then_inc(s_fold, 1)
            dve.tensor_copy(w1_hi[:], w1b_sb).then_inc(s_fold, 1)
            dve.wait_ge(s_fold, 4)
            dve.tensor_tensor(w1_lo[:], w1b_sb, w1_hi[:], ALU.subtract).then_inc(s_fold, 1)

            dve.wait_ge(s_gather, 16 * F)
            for k in range(2):
                reorder(dve, k)

            def pair(n, to, x0, x1):
                if not isinstance(n, int) or n >= RING:
                    dve.wait_ge(s_used, n - RING + 1)
                dve.tensor_tensor(prod[:, to, :, :], x0.unsqueeze(1).broadcast_to([P, 2, C]), x1,
                                  ALU.mult).then_inc(s_prod, 1)

            def layer0(g, r):
                c = KC * g + r
                s = r % 2
                dve.wait_ge(s_x4, 2 * (c + 1))
                dve.wait_ge(s_lo[s], 16 * G4 * ((KC // 2) * g + r // 2 + 1))
                for i in range(PAIRS0):
                    pair(pairs0(g, r, i), ring0(g, r, i), x4[:, s, :], xs_lo[:, s, 2 * i:2 * i + 2, :])
                dve.wait_ge(s_x16[s], 16 * ((KC // 2) * g + r // 2 + 1))
                if not (isinstance(g, int) and g == 0 and r == 0):
                    dve.wait_ge(s_p16u, c)
                for j in range(2):
                    last = dve.tensor_tensor(prod16[F * j:F * j + F, :], x4[0:F, s, HC * j:HC * j + HC],
                                             x16[:, s, HC * j:HC * j + HC], ALU.mult)
                    last.then_inc(s_p16, 1)

            def layer1(g, r, i, between=None):
                c = KC * g + r
                s = r % 2
                n = PAIRS1 * c + i
                if i == 0:
                    dve.wait_ge(s_hid, c + 1)
                if i == PAIRS1 // 2:
                    dve.wait_ge(s_hi, 16 * G4 * (c + 1))
                t = 2 * i
                xs = xs_lo[:, s, t:t + 2, :] if t < SLO else xs_hi[:, t - SLO:t - SLO + 2, :]
                if not isinstance(n, int) or n > 0:
                    dve.wait_ge(s_part_lo, n)
                dve.tensor_tensor(raw[:], hid[:, s, 1, :].unsqueeze(1).broadcast_to([P, 2, C]), xs,
                                  ALU.mult).then_inc(s_raw, 1)
                pair(pairs1(g, r, i), ring1(g, r, i), hid[:, s, 0, :], xs)
                if between:
                    between(g, r - 1)
                dve.wait_ge(s_part_hi, n + 1)
                if not isinstance(n, int) or n >= SRING:
                    dve.wait_ge(s_parts_used, n - SRING + 1)
                dve.tensor_tensor(part_lo[:, i % SRING, :, :], raw[:], part_hi[:, i % SRING, :, :],
                                  ALU.subtract).then_inc(s_part_lo, 1)

            def sum_direct(g, r):
                c = KC * g + r
                dve.wait_ge(s_z1e, c + 1)
                k = r % KC
                dve.tensor_reduce(dsum[:, k, :], direct[:, r % 2, :].rearrange("p (b d) -> p b d", d=DC),
                                  AX.X, ALU.add).then_inc(s_dsum, 1)
                if k == KC - 1:
                    dve.wait_ge(s_dsum, c + 1)
                    gb = g + r // KC
                    dve.tensor_reduce(feat[:, bass.ts(gb, P)], dsum[:].rearrange("p k b -> p b k"),
                                      AX.X, ALU.add).then_inc(s_feat, 1)

            def layer2(g, r):
                c = KC * g + r
                dve.wait_ge(s_q, c + 1)
                dve.wait_ge(s_xq[r % KC], 64 * (g + r // KC + 1))
                if not (isinstance(g, int) and g == 0 and r == 0):
                    dve.wait_ge(s_s, c)
                dve.tensor_tensor(qprod[:], q_ps[:, 0:Q4], xq[:, r % KC, :], ALU.mult).then_inc(s_qp, 1)

            def sum_z2(g, r):
                gb = g + r // KC
                dve.wait_ge(s_z2, KC * (gb + 1))
                dve.tensor_reduce(z2sum[:], z2[:].rearrange("p k (b d) -> p b k d", d=DC),
                                  AX.XY, ALU.add).then_inc(s_z2s, 1)
                dve.wait_ge(s_z2s, gb + 1)
                dve.tensor_tensor(feat_small[0:4, bass.ts(gb, P)].rearrange("p (j b) -> p j b", j=4),
                                  z2sum[:].unsqueeze(1).broadcast_to([4, 4, F]), mask[:],
                                  ALU.mult).then_inc(s_feat, 1)

            def stage(g, r):
                before, next1, _ = after(g, r)
                if next1:
                    layer0(g, r + 1)
                for i in range(PAIRS1):
                    layer1(g, r, i, {1: sum_direct, 2: layer2}.get(i) if before else None)
                    if i == 1 and (r - 2) % KC == KC - 1 and not (isinstance(g, int) and g == 0):
                        sum_z2(g, r - 2)

            layer0(0, 0)
            stages(dve, stage)
            sum_direct(NT - 1, KC - 1)
            layer2(NT - 1, KC - 1)
            sum_z2(NT - 1, KC - 1)

        @block.tensor
        def _(pe):
            def transposes(g, r, half):
                c = KC * g + r
                pe.wait_ge(s_emb, c + 1)
                two_banks = isinstance(g, int) and g == 0 and r < 2
                if not (two_banks and r == 0):
                    pe.wait_ge(s_x4, 2 * c + half - (1 if two_banks else 0))
                for i in range(DC // 2):
                    last = pe.transpose(t_bank(g, r, half)[:, i, :], emb[:, r % 2, half * DC // 2 + i, :, :].rearrange("p q f -> p (q f)"),
                                        ident[:])
                last.then_inc(s_t, 1)

            def matmuls(n, at, out, weights, start, stop):
                pe.wait_ge(s_prod, n + 1)
                for j in range(2):
                    for half in range(2):
                        last = pe.matmul(out[:, half, :], weights[j],
                                         prod[:, at, j, HC * half:HC * half + HC],
                                         start=start and j == 0, stop=stop and j == 1)
                last.then_inc(s_used, 1)
                return last

            def matmuls_parts(g, r, i):
                pe.wait_ge(s_part_lo, PAIRS1 * (KC * g + r) + i + 1)
                for j in range(2):
                    for w, p in ((w1_hi, part_hi), (w1_hi, part_lo), (w1_lo, part_hi)):
                        for half in range(2):
                            last = pe.matmul(z1_ps[:, half, :], w[:, 2 * i + j, :],
                                             p[:, i % SRING, j, HC * half:HC * half + HC], start=False,
                                             stop=i == PAIRS1 - 1 and j == 1 and w is w1_lo)
                last.then_inc(s_parts_used, 1)

            def layer0(g, r):
                c = KC * g + r
                if not (isinstance(g, int) and g == 0 and r == 0):
                    pe.wait_ge(s_z0e, c)
                for i in range(PAIRS0):
                    matmuls(pairs0(g, r, i), ring0(g, r, i), z0_ps, [w0_sb[:, 2 * i + j, :] for j in range(2)], i == 0, False)
                pe.wait_ge(s_p16, 2 * (c + 1))
                for half in range(2):
                    rows = slice(F * half, F * half + F)
                    last = pe.matmul(z0_ps[:, half, :], w0r_sb[rows, :], prod16[rows, :],
                                     start=False, stop=True)
                last.then_inc(s_p16u, 1)

            def layer2_q(g, r):
                c = KC * g + r
                pe.wait_ge(s_z1e, c + 1)
                if not (isinstance(g, int) and g == 0 and r == 0):
                    wait_apart(pe, s_qp, c)
                for j in range(4):
                    last = pe.matmul(q_ps[F * j:F * j + F, 0:Q4], w2_sb[H:P, :], h1[H:P, Q4 * j:Q4 * j + Q4],
                                     start=True, stop=True)
                last.then_inc(s_q, 1)

            def layer2_sum(g, r):
                c = KC * g + r
                pe.wait_ge(s_qp, c + 1)
                if not (isinstance(g, int) and g == 0 and r == 0):
                    pe.wait_ge(s_z2, c)
                pe.matmul(s_ps[0:4, 0:Q4], ones[:], qprod[:], start=True, stop=True).then_inc(s_s, 1)

            def stage(g, r):
                before, next1, next2 = after(g, r)
                if next2:
                    transposes(g, r + 2, 0)
                if next1:
                    layer0(g, r + 1)
                if next2:
                    transposes(g, r + 2, 1)
                c = KC * g + r
                if before:
                    pe.wait_ge(s_z1e, c)
                for i in range(PAIRS1):
                    matmuls(pairs1(g, r, i), ring1(g, r, i), z1_ps, [w1_sb[:, 2 * i + j, :] for j in range(2)],
                            i == 0, False)
                    if i == 1 and before:
                        layer2_q(g, r - 1)
                    if i == 3 and before:
                        layer2_sum(g, r - 1)
                    matmuls_parts(g, r, i)

            pe.wait_ge(s_w, 16 * 18)
            pe.wait_ge(s_fold, 5)
            for r in range(2):
                transposes(0, r, 0)
                transposes(0, r, 1)
            layer0(0, 0)
            stages(pe, stage)

            def tower1(n, i):
                lo, hi = TB[n]
                if n:
                    pe.wait_ge(s_m1e, U1 // P)
                pe.matmul(bank1(i)[:, lo:hi], wt1a_sb[:, P * i:P * i + P], feat[:, lo:hi],
                          start=True, stop=False)
                pe.wait_ge(s_feat, 2 * hi // P)
                pe.matmul(bank1(i)[:, lo:hi], wt1b_sb[:, P * i:P * i + P], feat_small[:, lo:hi],
                          start=False, stop=True).then_inc(s_m1, 1)

            def tower2(n):
                lo, hi = TB[n]
                if n:
                    pe.wait_ge(s_m2e, U2 // P)
                for i in range(U2 // P):
                    for k in range(U1 // P):
                        if i == 0:
                            pe.wait_ge(s_m1e, U1 // P * n + k + 1)
                        last = pe.matmul(bank2(i)[:, lo:hi], wt2_sb[:, k, P * i:P * i + P], hid1[:, k, lo:hi],
                                         start=(k == 0), stop=(k == U1 // P - 1))
                    last.then_inc(s_m2, 1)

            def tower3(n):
                lo, hi = TB[n]
                pe.wait_ge(s_m2e, U2 // P * (n + 1))
                for t in range(lo // P, hi // P):
                    for k in range(U2 // P):
                        last = pe.matmul(s_ps[:, t:t + 1], hid2[:, k, P * t:P * t + P], wt3_sb[:, k:k + 1],
                                         start=(k == 0), stop=(k == U2 // P - 1))
                return last

            pe.wait_ge(s_z0e, NCH)
            pe.wait_ge(s_feat, 2 * (NT - 1))
            tower1(0, 0)
            tower1(0, 1)
            layer2_q(NT - 1, KC - 1)
            tower1(0, 2)
            tower1(0, 3)
            layer2_sum(NT - 1, KC - 1)
            tower2(0)
            pe.wait_ge(s_feat, 2 * NT - 1)
            for i in range(U1 // P):
                tower1(1, i)
            pe.wait_ge(s_z2, NCH)
            tower3(0)
            tower2(1)
            tower3(1).then_inc(s_y, 1)


def kernel(**inputs):
    import numpy as np
    import concourse.bacc as bacc
    from concourse.bass_utils import run_bass_kernel_spmd

    a = {k: np.asarray(v) for k, v in inputs.items()}
    l = np.arange(F)
    q = np.arange(G4)[:, None]
    w0 = a["L0_rec_W0"].reshape(O, F, F)
    m = (l + q + G4 * np.arange(NS)[:, None, None]) % F
    mo = m[:SLO].transpose(1, 2, 0)
    ll = np.broadcast_to(l[None, :, None], mo.shape)
    w0a = w0[:, ll, mo].transpose(1, 2, 3, 0).reshape(P, SLO, O)
    w0b = w0[:, mo, ll].transpose(1, 2, 3, 0).reshape(P, SLO, O)
    w0r = w0[:, l, (l + F // 2) % F].T
    w1 = a["L0_rec_W1"].reshape(O, H, F)
    order = np.r_[H:O, 0:H]
    mm = np.broadcast_to(m.transpose(1, 2, 0)[..., None], (G4, F, NS, 2))
    hh = F * ((q[:, :, None, None] + np.arange(2)) % 2) + l[None, :, None, None]
    w1t = w1[order][:, np.broadcast_to(hh, mm.shape), mm].transpose(1, 2, 4, 3, 0).reshape(P, 2, NS, O)
    wt1 = a["W_top1"]
    arrays = {
        "ids": a["ids"].reshape(P, NT, F).transpose(1, 0, 2),
        "dense_t": a["dense_ctx"].reshape(P, NT, NDENSE).transpose(2, 1, 0).reshape(NDENSE, B),
        "w0a": w0a, "w0b": w0b, "w0r": np.concatenate([w0r, w0r]), "w1": w1t,
        "w2": a["L0_rec_W2"].reshape(H, F),
        "bias_cin": np.stack([a["L0_rec_b0"], a["L0_rec_b1"][order]], axis=1),
        "b2": np.repeat(a["L0_rec_b2"].reshape(1, 1), 4, axis=0),
        "wt1a": wt1[order], "wt1b": np.concatenate([np.repeat(wt1[O:O + 1], 4, axis=0), wt1[O + 1:]]),
        "bt1": a["b_top1"].reshape(U1 // P, P).T,
        "wt2": a["W_top2"].reshape(U1 // P, P, U2).transpose(1, 0, 2),
        "bt2": a["b_top2"].reshape(U2 // P, P).T, "wt3": a["W_top3"].reshape(U2 // P, P).T,
        "ident": np.eye(P, dtype=np.float32),
        "ones": np.repeat(np.eye(4, dtype=np.float32), F, axis=0),
        "mask": np.repeat(np.eye(4, dtype=np.float32), F, axis=1).reshape(4, 4, F),
    }
    arrays = {k: np.ascontiguousarray(v) for k, v in arrays.items()}
    tables = {f"tbl_{f}": a[f"tbl_{f}"] for f in range(F)}

    nc = bacc.Bacc("TRN2", target_bir_lowering=False, num_devices=1)

    def dram(name, x):
        return nc.dram_tensor(f"in_{name}", x.shape, mybir.dt.from_np(x.dtype), kind="ExternalInput").ap()
    tabs = [dram(k, v) for k, v in tables.items()]
    args = [dram(k, v) for k, v in arrays.items()]
    y = nc.dram_tensor("out_y", (B, 1), F32, kind="ExternalOutput").ap()
    build(nc, tabs, *args, y)
    feeds = {f"in_{k}": v for k, v in {**tables, **arrays}.items()}
    r = run_bass_kernel_spmd(nc, [feeds], core_ids=[0])
    return r.results[0]["out_y"]
```

```python
from contextlib import ExitStack

import concourse.bass as bass
from concourse import mybir

F32 = mybir.dt.float32
F32R = mybir.dt.float32r
I32 = mybir.dt.int32
ALU = mybir.AluOpType
ACT = mybir.ActivationFunctionType
AX = mybir.AxisListType

B, F, D = 512, 32, 32
H = 64
O = 2 * H
NDENSE = 16
U1, U2 = 512, 256

P = 128
NB = 32
NCH = B // NB
KC = 4
NG = NCH // KC
C = NB * D
HC = C // 2
Q4 = C // 4
NBQ = NB // 4
G4 = P // F
NT = B // P
NS = F // G4
SLO = NS // 2
RING = 2
SRING = 2
RAWS = 2
PAIRS0 = SLO // 2
PAIRS1 = NS // 2
PAIRS = PAIRS0 + PAIRS1
ODD = 0
XQR = 4



def build(nc, table, ids, first_row, dense_t, w0a, w0b, w16, w1, w2, bias_cin, b2, wt1a, wt1b, bt1,
          wt2, bt2, wt3, ones_in, mask_in, signs_in, y_out):
    scratch = nc.dram_tensor("x_fields", (NCH, 2 * F, C), F32).ap()

    with ExitStack() as ctx:
        def sb(name, shape, dt=F32):
            return ctx.enter_context(nc.sbuf_tensor(name, shape, dt))

        def ps(name, shape):
            return ctx.enter_context(nc.psum_tensor(name, shape, F32))

        def sem(name):
            return ctx.enter_context(nc.semaphore(name))

        ids_sb = sb("ids_sb", [P, NCH, NBQ], I32)
        first_row_sb = sb("first_row_sb", [P, 1], I32)
        rows_sb = sb("rows_sb", [P, NCH, NBQ], I32)
        rows_now = sb("rows_now", [P, KC, NBQ], I32)
        gathered = sb("gathered", [P, XQR, NBQ, D])
        x4 = sb("x4", [P, 2, C])
        xs_lo = sb("xs_lo", [P, 2, SLO, C])
        xs_hi = sb("xs_hi", [P, SLO, C])
        xq = sb("xq", [P, XQR, Q4])
        xq16 = sb("xq16", [P, 2, Q4])
        hid = sb("hid", [P, 2, 2, C])
        prod = sb("prod", [P, RING, 2, C])
        raw = sb("raw", [P, RAWS, 2, C])
        part_hi = sb("part_hi", [P, SRING, 2, C], F32R)
        part_lo = sb("part_lo", [P, SRING, 2, C], F32R)
        prod16 = sb("prod16", [P, Q4])
        round16 = sb("round16", [P, Q4], F32R)
        parts16 = sb("parts16", [P, Q4], F32R)
        direct = sb("direct", [P, 2, C])
        h1 = sb("h1", [P, C])
        qprod = sb("qprod", [P, Q4])
        z2 = sb("z2", [4, Q4])
        z2sum = sb("z2sum", [4, NCH, NBQ])
        feat = sb("feat", [P, B])
        feat_small = sb("feat_small", [4 + NDENSE, B])
        hid1 = x4[:].rearrange("p s (i b) -> p (s i) b", b=B)
        hid2 = hid[:, 0, 0, :].rearrange("p (i b) -> p i b", b=B)
        y_sb = sb("y_sb", [P, NT])
        w0_sb = sb("w0_sb", [P, SLO, O])
        w0b_sb = raw[:, 0, 0, 0:SLO * O].rearrange("p (t o) -> p t o", o=O)
        w16_sb = sb("w16_sb", [P, 2, O])
        w16_round = sb("w16_round", [P, O], F32R)
        w16_rest = sb("w16_rest", [P, O])
        w16_hi = sb("w16_hi", [P, G4, O], F32R)
        w16_lo = sb("w16_lo", [P, G4, O], F32R)
        signs = sb("signs", [P, 1 + 2 * G4])
        w1_sb = sb("w1_sb", [P, NS, O])
        w1_hi = sb("w1_hi", [P, NS, O], F32R)
        w1_lo = sb("w1_lo", [P, NS, O], F32R)
        w1_odd = sb("w1_odd", [P, O])
        w1b_sb = hid[:, 0, 0, :].rearrange("p (t o) -> p t o", o=O)
        w2_sb = sb("w2_sb", [P, F])
        bias_sb = sb("bias_sb", [P, 2])
        b2_sb = sb("b2_sb", [4, 1])
        wt1a_sb = sb("wt1a_sb", [P, U1])
        wt1b_sb = sb("wt1b_sb", [4 + NDENSE, U1])
        bt1_sb = sb("bt1_sb", [P, U1 // P])
        wt2_sb = sb("wt2_sb", [P, U1 // P, U2])
        bt2_sb = sb("bt2_sb", [P, U2 // P])
        wt3_sb = sb("wt3_sb", [P, U2 // P])
        ones = sb("ones", [P, 4])
        mask = sb("mask", [4, 4, NBQ])

        z0_ps = ps("z0_ps", [P, 2, HC])
        z1_ps = ps("z1_ps", [P, 2, HC])
        more_ps = ps("more_ps", [P, 512])
        q_ps = ps("q_ps", [P, 512])
        z0b_ps = ps("z0b_ps", [P, 2, HC])
        s_ps = z0b_ps[:, 0, :]

        loads = [(w0_sb[:], w0a), (w0b_sb, w0b), (w16_sb[:], w16), (signs[:], signs_in),
                 (bias_sb[:], bias_cin), (w1_sb[:], w1[:, 0, :, :]), (w1b_sb, w1[:, 1, :, :]),
                 (w1_odd[:], w1[:, 1, 2 * ODD + 1, :]), (w2_sb[H:P, :], w2), (b2_sb[:], b2),
                 (ones[:], ones_in), (mask[:], mask_in), (feat_small[4:4 + NDENSE, :], dense_t),
                 (wt1a_sb[:], wt1a), (wt1b_sb[:], wt1b), (bt1_sb[:], bt1), (wt2_sb[:], wt2),
                 (bt2_sb[:], bt2), (wt3_sb[:], wt3)]
        NLOADS = len(loads)

        s_w = sem("w_loaded")
        s_ids = sem("ids_loaded")
        s_rows = sem("rows_ready")
        s_rows_now = sem("rows_now_ready")
        s_gather = [sem(f"rows_gathered{i}") for i in range(XQR)]
        s_x4 = [sem(f"x4_loaded{i}") for i in range(2)]
        s_store = [sem(f"x_stored{i}") for i in range(2)]
        s_lo = [sem(f"lo_loaded{i}") for i in range(2)]
        s_hi = sem("hi_loaded")
        s_xq16 = [sem(f"xq16_loaded{i}") for i in range(2)]
        s_xq = [sem(f"xq_loaded{i}") for i in range(XQR)]
        s_lo_pair0 = [sem(f"lo_pair0_loaded{i}") for i in range(2)]
        s_fold = sem("weights_ready")
        s_prod = sem("prod_ready")
        s_used = sem("prod_used")
        s_raw = sem("raw_ready")
        s_part_hi = sem("part_hi_ready")
        s_part_lo = sem("part_lo_ready")
        s_parts_used = sem("parts_used")
        s_p16 = sem("prod16_ready")
        s_round16 = sem("round16_ready")
        s_parts16 = sem("parts16_ready")
        s_p16u = sem("parts16_used")
        s_hid = sem("hid_ready")
        s_z0e = sem("z0_copied")
        s_direct = sem("direct_ready")
        s_z1e = sem("z1_copied")
        s_q = sem("q_ready")
        s_qp = sem("qprod_ready")
        s_s = sem("s_ready")
        s_z2 = sem("z2_ready")
        s_dsum = sem("dsum_ready")
        s_z2s = sem("z2sum_ready")
        s_spread = sem("z2sum_spread")
        s_m1 = sem("tower1_ready")
        s_m1e = sem("tower1_copied")
        s_m2 = sem("tower2_ready")
        s_m2e = sem("tower2_copied")
        s_y = sem("y_ready")
        s_ye = sem("y_copied")
        s_out = sem("y_stored")
        s_table = sem("table_loaded")
        s_apart = sem("waits_apart")

        def halves(i):
            return 3 if i == ODD else 4

        def flat(buffers, at, i):
            return buffers[:, at, :, :].rearrange("p j n -> p (j n)")[:, 0:HC * halves(i)]

        def pairs0(g, r, i):
            return i if isinstance(g, int) and KC * g + r == 0 else PAIRS * (KC * g + r - 1) + PAIRS0 + i

        def pairs1(g, r, i):
            last = isinstance(g, int) and KC * g + r == NCH - 1
            return PAIRS * (KC * g + r) + PAIRS0 + i + (0 if last else PAIRS0)

        def ring0(g, r, i):
            return (pairs0(0, r, i) if isinstance(g, int) and g == 0 else PAIRS * (r - 1) + PAIRS0 + i) % RING

        def ring1(g, r, i):
            return (pairs1(g, r, i) if isinstance(g, int) else pairs1(0, r, i)) % RING

        TB = [(0, B - 2 * NB), (B - 2 * NB, B)]

        def bank1(n, i):
            z0, z1 = ([z[:, j, :] for j in range(2)] for z in (z0_ps, z1_ps))
            more = [more_ps[:], z0b_ps[:, 1, :]]
            return (more + z0 if n else z1 + more)[i]

        def bank2(i):
            return z1_ps[:, i, :]

        def z1_banks(g, r):
            return z0_ps if isinstance(g, int) and KC * g + r == NCH - 1 else z1_ps

        def z0_banks(g, r):
            return z0b_ps if isinstance(g, int) and g == 0 and r == 1 else z0_ps

        def wait_apart(eng, semaphore, value):
            eng.wait_ge(semaphore, value)
            eng.sem_inc(s_apart, 1)

        block = ctx.enter_context(nc.Block())

        def stages(eng, stage):
            stage(0, 0)
            stage(0, 1)
            with eng.Fori(0, NG - 1) as g:
                for r in range(2, 2 + KC):
                    stage(g, r)
            stage(NG - 1, 2)
            stage(NG - 1, 3)

        def after(g, r):
            last = isinstance(g, int) and g == NG - 1 and r == KC - 1
            return not (isinstance(g, int) and g == 0 and r == 0), not last

        @block.gpsimd
        def _(pool):
            def gather(g, k, rows):
                for i in range(NBQ):
                    pool.indirect_dma_start(
                        out=gathered[:, k, i, :], out_offset=None, in_=table,
                        in_offset=bass.IndirectOffsetOnAxis(ap=rows[:, i:i + 1], axis=0),
                    ).then_inc(s_gather[k], 16)

            pool.wait_ge(s_rows, 1)
            for k in range(KC):
                gather(0, k, rows_sb[:, k, :])
            with pool.Fori(1, NG) as g:
                for k in range(KC):
                    wait_apart(pool, s_gather[k], 16 * NBQ * g)
                pool.tensor_copy(rows_now[:], rows_sb[:, bass.ts(g, KC), :]).then_inc(s_rows_now, 1)
                wait_apart(pool, s_rows_now, g)
                for k in range(KC):
                    wait_apart(pool, s_store[k % 2], 32 * ((KC // 2) * (g - 1) + k // 2 + 1))
                    gather(g, k, rows_now[:, k, :])

        @block.sync
        def _(sp):
            def shifted(c, at, tiles):
                row = scratch[bass.ds(c, 1), at:at + 1, 0:1]
                return bass.AP(row.tensor, row.offset, [[C, F], [G4 * C, tiles], [1, C]],
                               runtime_checks=row.runtime_checks)

            def store(g, k):
                c = KC * g + k
                wait_apart(sp, s_gather[k], 16 * NBQ * (g + 1))
                for i in range(2):
                    sp.dma_start(stored(c)[F * i:F * i + F, :].rearrange("l (q n) -> (l q) n", n=Q4),
                                 gathered[:, k, :, :].rearrange("p i d -> p (i d)")).then_inc(s_store[k % 2], 16)

            def wait_stored(g, k):
                wait_apart(sp, s_store[k % 2], 32 * ((KC // 2) * g + k // 2 + 1))

            def stored(c):
                return scratch[bass.ds(c, 1), :, :].rearrange("a m n -> (a m) n")

            def load_x4(c, p):
                for q in range(G4):
                    sp.dma_start(x4[F * q:F * q + F, p, :], stored(c)[0:F, :]).then_inc(s_x4[p], 16)

            def load_lo(c, p, lo, hi, loaded):
                for q in range(G4):
                    sp.dma_start(xs_lo[F * q:F * q + F, p, lo:hi, :],
                                 shifted(c, G4 * lo + q, hi - lo)).then_inc(loaded, 16)

            def load_xq(c, k, shift, to, loaded):
                for j in range(4):
                    sp.dma_start(to[F * j:F * j + F, k, :],
                                 stored(c)[shift:shift + F, Q4 * j:Q4 * j + Q4]).then_inc(loaded[k], 16)

            def spread(g, k):
                c = KC * g + k
                store(g, k)
                wait_stored(g, k)
                wait_apart(sp, s_prod, pairs1(g, k - 2, PAIRS1 // 2))
                load_x4(c, k % 2)
                load_lo(c, k % 2, 0, SLO, s_lo[k % 2])
                wait_apart(sp, s_p16, c - 1)
                load_xq(c, k % 2, F // 2, xq16, s_xq16)
                if not isinstance(g, int):
                    wait_apart(sp, s_qp, c - 3)
                load_xq(c, k, 0, xq, s_xq)
                spread_hi(g, k - 1)

            def spread_hi(g, r):
                c = KC * g + r
                if not isinstance(g, int) or c > 0:
                    wait_apart(sp, s_prod, pairs1(g, r - 1, PAIRS1))
                for q in range(G4):
                    sp.dma_start(xs_hi[F * q:F * q + F, :, :],
                                 shifted(c, G4 * SLO + q, SLO)).then_inc(s_hi, 16)

            sp.dma_start(ids_sb[:], ids).then_inc(s_ids, 16)
            sp.dma_start(first_row_sb[:], first_row).then_inc(s_ids, 16)
            store(0, 0)
            for c in range(2):
                wait_stored(0, c)
                load_x4(c, c)
                load_lo(c, c, 0, 2, s_lo_pair0[c])
                load_lo(c, c, 2, SLO, s_lo[c])
                if c == 0:
                    store(0, 1)
                load_xq(c, c, F // 2, xq16, s_xq16)
                load_xq(c, c, 0, xq, s_xq)
            spread_hi(0, 0)
            for k in range(2, KC):
                spread(0, k)
            with sp.Fori(1, NG) as g:
                for k in range(KC):
                    spread(g, k)
            spread_hi(NG - 1, KC - 1)
            sp.wait_ge(s_ye, 1)
            sp.dma_start(y_out.rearrange("(p t) o -> p (t o)", t=NT), y_sb[:]).then_inc(s_out, 16)
            sp.wait_ge(s_out, 16)

        @block.scalar
        def _(act):
            for dst, src in loads:
                act.dma_start(dst, src).then_inc(s_w, 16)

            def round_16(g, r):
                act.wait_ge(s_p16, KC * g + r + 1)
                nc.scalar.activation(round16[:], prod16[:], ACT.Copy).then_inc(s_round16, 1)

            def round_part(g, r, i):
                n = PAIRS1 * (KC * g + r) + i
                act.wait_ge(s_raw, n + 1)
                if not isinstance(n, int) or n >= SRING:
                    act.wait_ge(s_parts_used, n - SRING + 1)
                nc.scalar.activation(flat(part_hi, i % SRING, i), flat(raw, i % RAWS, i),
                                     ACT.Copy).then_inc(s_part_hi, 1)

            def copy_z0(g, r, rounds):
                c = KC * g + r
                s = r % 2
                act.wait_ge(s_p16u, c + 1)
                if not (isinstance(g, int) and g == 0 and r < 2):
                    act.wait_ge(s_prod, pairs1(g, r - 2, PAIRS1))
                z = z0_banks(g, r)[:].rearrange("p h n -> p (h n)")

                def relu(out, lo, n):
                    return nc.scalar.activation(out, z[lo:lo + n, :], ACT.Relu, bias=bias_sb[lo:lo + n, 0:1])

                def variant_a():
                    relu(hid[0:H, s, 0, :], 0, H)
                    relu(hid[H:P, s, 0, :], 0, H).then_inc(s_hid, 1)

                def variant_b():
                    for q in range(G4):
                        last = relu(hid[F * q:F * q + F, s, 1, :], F * ((q + 1) % 2), F)
                    last.then_inc(s_hid, 1)

                if rounds:
                    variant_a()
                    round_part(g, r - 1, 1)
                    variant_b()
                else:
                    variant_b()
                    variant_a()
                if not (isinstance(g, int) and g == 0 and r < 2):
                    act.wait_ge(s_dsum, c - 1)
                relu(direct[H:P, s, :], H, H).then_inc(s_z0e, 1)

            def copy_z1(g, r):
                c = KC * g + r
                act.wait_ge(s_parts_used, PAIRS1 * (c + 1))
                z = z1_banks(g, r)[:].rearrange("p h n -> p (h n)")
                nc.scalar.activation(direct[0:H, r % 2, :], z[0:H, :], ACT.Relu,
                                     bias=bias_sb[0:H, 1:2]).then_inc(s_direct, 1)
                if after(g, r)[0]:
                    act.wait_ge(s_q, c)
                nc.scalar.activation(h1[H:P, :], z[H:P, :], ACT.Relu, bias=bias_sb[H:P, 1:2]).then_inc(s_z1e, 1)

            def copy_z2(g, r):
                c = KC * g + r
                act.wait_ge(s_s, c + 1)
                if not (isinstance(g, int) and g == 0 and r == 0):
                    act.wait_ge(s_z2s, c)
                nc.scalar.activation(z2[:], s_ps[0:4, 0:Q4], ACT.Relu,
                                     bias=b2_sb[:, 0:1]).then_inc(s_z2, 1)

            def copy_tower(n, i, bank, dst, width, bias, ready, copied):
                lo, hi = TB[n]
                act.wait_ge(ready, width // P * n + i + 1)
                nc.scalar.activation(dst[:, i, lo:hi], bank[:, lo:hi], ACT.Relu,
                                     bias=bias[:, i:i + 1]).then_inc(copied, 1)

            def copy_tower1(n, i):
                copy_tower(n, i, bank1(n, i), hid1, U1, bt1_sb, s_m1, s_m1e)

            def copy_tower2(n, i):
                copy_tower(n, i, bank2(i), hid2, U2, bt2_sb, s_m2, s_m2e)

            def stage(g, r):
                before, next1 = after(g, r)
                if next1:
                    round_16(g, r + 1)
                    round_part(g, r, 0)
                    copy_z0(g, r + 1, True)
                else:
                    round_part(g, r, 1)
                for i in range(2, PAIRS1):
                    if not next1:
                        copy_tower1(0, 2 * i - 4)
                        copy_tower1(0, 2 * i - 3)
                    round_part(g, r, i)
                if before:
                    copy_z2(g, r - 1)
                if isinstance(g, int) and KC * g + r == NCH - 2:
                    round_part(g, r + 1, 0)
                copy_z1(g, r)

            act.wait_ge(s_w, 16 * NLOADS)
            nc.scalar.activation(y_sb[:, 0:1], bias_sb[:, 0:1], ACT.Relu).then_inc(s_table, 1)
            round_16(0, 0)
            copy_z0(0, 0, False)
            stages(act, stage)

            copy_tower2(0, 0)
            copy_z2(NG - 1, KC - 1)
            copy_tower2(0, 1)
            for i in range(U1 // P):
                copy_tower1(1, i)
            for i in range(U2 // P):
                copy_tower2(1, i)
            act.wait_ge(s_y, 1)
            nc.scalar.activation(y_sb[:], s_ps[:, 0:NT], ACT.Copy).then_inc(s_ye, 1)

        @block.vector
        def _(dve):
            dve.wait_ge(s_ids, 32)
            dve.tensor_tensor(rows_sb[:].rearrange("p c i -> p (c i)"), ids_sb[:].rearrange("p c i -> p (c i)"),
                              first_row_sb[:].broadcast_to([P, NCH * NBQ]), ALU.add).then_inc(s_rows, 1)

            dve.wait_ge(s_w, 16 * NLOADS)
            for at in ((slice(F, 2 * F), slice(0, 1)), (slice(2 * F, P), slice(0, 1)), (slice(0, P), slice(1, SLO))):
                dve.tensor_tensor(w0_sb[at[0], at[1], :], w0_sb[at[0], at[1], :], w0b_sb[at[0], at[1], :],
                                  ALU.add).then_inc(s_fold, 1)
            dve.tensor_copy(w1_hi[:], w1b_sb).then_inc(s_fold, 1)
            dve.tensor_tensor(w16_sb[:, 0, :], w16_sb[:, 0, :], w16_sb[:, 1, :], ALU.add).then_inc(s_fold, 1)
            dve.wait_ge(s_fold, 5)
            dve.tensor_tensor(w1_lo[:], w1b_sb, w1_hi[:], ALU.subtract).then_inc(s_fold, 1)
            dve.tensor_copy(w16_round[:], w16_sb[:, 0, :]).then_inc(s_fold, 1)
            dve.wait_ge(s_fold, 7)
            dve.tensor_tensor(w16_rest[:], w16_sb[:, 0, :], w16_round[:], ALU.subtract).then_inc(s_fold, 1)

            def signed(to, w, at):
                dve.tensor_tensor(to[:], w[:].unsqueeze(1).broadcast_to([P, G4, O]),
                                  signs[:, at:at + G4].unsqueeze(2).broadcast_to([P, G4, O]),
                                  ALU.mult).then_inc(s_fold, 1)

            signed(w16_hi, w16_round, 1)
            dve.wait_ge(s_fold, 9)
            signed(w16_lo, w16_rest, 1 + G4)

            def pair(n, to, x0, x1):
                if not isinstance(n, int) or n >= RING:
                    dve.wait_ge(s_used, n - RING + 1)
                dve.tensor_tensor(prod[:, to, :, :], x0.unsqueeze(1).broadcast_to([P, 2, C]), x1,
                                  ALU.mult).then_inc(s_prod, 1)

            def layer0(g, r):
                c = KC * g + r
                s = r % 2
                dve.wait_ge(s_x4[s], 64 * ((KC // 2) * g + r // 2 + 1))
                first = isinstance(g, int) and g == 0
                for i in range(PAIRS0):
                    if first and r < 2 and i == 0:
                        dve.wait_ge(s_lo_pair0[r], 16 * G4)
                    else:
                        dve.wait_ge(s_lo[s], 16 * G4 * ((KC // 2) * g + r // 2 + 1))
                    pair(pairs0(g, r, i), ring0(g, r, i), x4[:, s, :], xs_lo[:, s, 2 * i:2 * i + 2, :])
                dve.wait_ge(s_xq16[s], 64 * ((KC // 2) * g + r // 2 + 1))
                dve.wait_ge(s_xq[r % KC], 64 * (g + r // KC + 1))
                if not (first and r == 0):
                    dve.wait_ge(s_parts16, c)
                dve.tensor_tensor(prod16[:], xq[:, r % KC, :], xq16[:, s, :], ALU.mult).then_inc(s_p16, 1)

            def parts_16(g, r):
                c = KC * g + r
                dve.wait_ge(s_round16, c + 1)
                if not (isinstance(g, int) and g == 0 and r == 0):
                    dve.wait_ge(s_p16u, c)
                dve.scalar_tensor_tensor(parts16[:], prod16[:], signs[:, 0:1], round16[:],
                                         ALU.mult, ALU.subtract).then_inc(s_parts16, 1)

            def layer1(g, r, i):
                c = KC * g + r
                s = r % 2
                n = PAIRS1 * c + i
                if i == 0:
                    first = isinstance(g, int) and c == 0
                    dve.wait_ge(s_hid, 1 if first else 2 * c + 2)
                if i == PAIRS1 // 2:
                    dve.wait_ge(s_hi, 16 * G4 * (c + 1))
                t = 2 * i
                xs = xs_lo[:, s, t:t + 2, :] if t < SLO else xs_hi[:, t - SLO:t - SLO + 2, :]
                if not isinstance(n, int) or n >= RAWS:
                    dve.wait_ge(s_part_lo, n - RAWS + 1)
                    if (i - RAWS) % PAIRS1 == ODD:
                        dve.wait_ge(s_parts_used, n - RAWS + 1)
                dve.tensor_tensor(raw[:, i % RAWS, :, :], hid[:, s, 1, :].unsqueeze(1).broadcast_to([P, 2, C]),
                                  xs, ALU.mult).then_inc(s_raw, 1)
                if isinstance(g, int) and c == 0 and i == 0:
                    dve.wait_ge(s_hid, 2)
                before, next1 = after(g, r)
                if i == 0 and next1:
                    parts_16(g, r + 1)
                    if before:
                        sum_direct(g, r - 1)
                        if not (isinstance(g, int) and g == 0 and r == 1):
                            sum_z2(g, r - 2)
                pair(pairs1(g, r, i), ring1(g, r, i), hid[:, s, 0, :], xs)
                if i == 1 and not next1:
                    sum_z2(g, r - 2)
                    spread_z2(0)
                    sum_direct(g, r - 1)
                if before and i == 2:
                    layer2(g, r - 1)
                dve.wait_ge(s_part_hi, n + 1)
                if not isinstance(n, int) or n >= SRING:
                    dve.wait_ge(s_parts_used, n - SRING + 1)
                dve.tensor_tensor(flat(part_lo, i % SRING, i), flat(raw, i % RAWS, i),
                                  flat(part_hi, i % SRING, i), ALU.subtract).then_inc(s_part_lo, 1)

            def sum_direct(g, r):
                c = KC * g + r
                dve.wait_ge(s_direct, c + 1)
                dve.tensor_reduce(feat[:, bass.ts(c, NB)], direct[:, r % 2, :].rearrange("p (b d) -> p b d", d=D),
                                  AX.X, ALU.add).then_inc(s_dsum, 1)

            def layer2(g, r):
                c = KC * g + r
                dve.wait_ge(s_q, c + 1)
                dve.wait_ge(s_xq[r % KC], 64 * (g + r // KC + 1))
                if not (isinstance(g, int) and g == 0 and r == 0):
                    dve.wait_ge(s_s, c)
                dve.tensor_tensor(qprod[:], q_ps[:, 0:Q4], xq[:, r % KC, :], ALU.mult).then_inc(s_qp, 1)

            def sum_z2(g, r):
                c = KC * g + r
                dve.wait_ge(s_z2, c + 1)
                dve.tensor_reduce(z2sum[:, bass.ds(c, 1), :].rearrange("p a b -> p (a b)"),
                                  z2[:].rearrange("p (b d) -> p b d", d=D),
                                  AX.X, ALU.add).then_inc(s_z2s, 1)

            def spread_z2(n):
                lo, hi = TB[n]
                dve.wait_ge(s_z2s, hi // NB)
                shape = [4, (hi - lo) // NB, 4, NBQ]
                dve.tensor_tensor(feat_small[0:4, lo:hi].rearrange("p (c j b) -> p c j b", j=4, b=NBQ),
                                  z2sum[:, lo // NB:hi // NB, :].unsqueeze(2).broadcast_to(shape),
                                  mask[:].unsqueeze(1).broadcast_to(shape), ALU.mult).then_inc(s_spread, 1)

            def stage(g, r):
                if after(g, r)[1]:
                    layer0(g, r + 1)
                for i in range(PAIRS1):
                    layer1(g, r, i)

            layer0(0, 0)
            parts_16(0, 0)
            stages(dve, stage)
            sum_z2(NG - 1, KC - 2)
            sum_direct(NG - 1, KC - 1)
            layer2(NG - 1, KC - 1)
            sum_z2(NG - 1, KC - 1)
            spread_z2(1)

        @block.tensor
        def _(pe):
            def matmuls(n, at, out, weights, start, stop):
                pe.wait_ge(s_prod, n + 1)
                for j in range(2):
                    for half in range(2):
                        last = pe.matmul(out[:, half, :], weights[j],
                                         prod[:, at, j, HC * half:HC * half + HC],
                                         start=start and j == 0, stop=stop and j == 1)
                last.then_inc(s_used, 1)

            def matmuls_parts(g, r, i):
                def product(j, half, w, p, at, ends=False):
                    return pe.matmul(z1_banks(g, r)[:, half, :], w, p[:, at, j, HC * half:HC * half + HC],
                                     start=False, stop=ends)

                pe.wait_ge(s_part_lo, PAIRS1 * (KC * g + r) + i + 1)
                for j in range(2):
                    split = [half for half in range(2) if 2 * j + half < halves(i)]
                    for w, p in ((w1_hi, part_hi), (w1_hi, part_lo), (w1_lo, part_hi)):
                        for half in split:
                            last = product(j, half, w[:, 2 * i + j, :], p, i % SRING,
                                           i == PAIRS1 - 1 and j == 1 and w is w1_lo)
                if i == ODD:
                    last = product(1, 1, w1_odd[:], raw, i % RAWS)
                last.then_inc(s_parts_used, 1)

            def layer0(g, r):
                c = KC * g + r
                if not (isinstance(g, int) and g == 0 and r < 2):
                    pe.wait_ge(s_z0e, c)
                for i in range(PAIRS0):
                    matmuls(pairs0(g, r, i), ring0(g, r, i), z0_banks(g, r),
                            [w0_sb[:, 2 * i + j, :] for j in range(2)], i == 0, False)
                pe.wait_ge(s_parts16, c + 1)
                for w in (w16_hi, w16_lo):
                    for j in range(4):
                        last = pe.matmul(z0_banks(g, r)[:, j // 2, Q4 * (j % 2):Q4 * (j % 2) + Q4], w[:, j, :],
                                         parts16[:], start=False, stop=w is w16_lo and j % 2 == 1)
                last.then_inc(s_p16u, 1)

            def layer2_q(g, r):
                c = KC * g + r
                pe.wait_ge(s_z1e, c + 1)
                if not (isinstance(g, int) and g == 0 and r == 0):
                    wait_apart(pe, s_qp, c)
                for j in range(4):
                    last = pe.matmul(q_ps[F * j:F * j + F, 0:Q4], w2_sb[H:P, :], h1[H:P, Q4 * j:Q4 * j + Q4],
                                     start=True, stop=True)
                last.then_inc(s_q, 1)

            def layer2_sum(g, r):
                c = KC * g + r
                pe.wait_ge(s_qp, c + 1)
                if not (isinstance(g, int) and g == 0 and r == 0):
                    pe.wait_ge(s_z2, c)
                pe.matmul(s_ps[0:4, 0:Q4], ones[:], qprod[:], start=True, stop=True).then_inc(s_s, 1)

            def tower1(n, i):
                lo, hi = TB[n]
                pe.wait_ge(s_dsum, hi // NB)
                pe.matmul(bank1(n, i)[:, lo:hi], wt1a_sb[:, P * i:P * i + P], feat[:, lo:hi],
                          start=True, stop=False)
                pe.wait_ge(s_spread, n + 1)
                pe.matmul(bank1(n, i)[:, lo:hi], wt1b_sb[:, P * i:P * i + P], feat_small[:, lo:hi],
                          start=False, stop=True).then_inc(s_m1, 1)

            def stage(g, r):
                before, next1 = after(g, r)
                if next1:
                    layer0(g, r + 1)
                c = KC * g + r
                if not next1:
                    pe.wait_ge(s_z0e, NCH)
                elif before:
                    pe.wait_ge(s_z1e, c)
                for i in range(PAIRS1):
                    if not next1 and i in (1, 2):
                        pe.wait_ge(s_z1e, c)
                        tower1(0, 2 * i - 2)
                        tower1(0, 2 * i - 1)
                    matmuls(pairs1(g, r, i), ring1(g, r, i), z1_banks(g, r),
                            [w1_sb[:, 2 * i + j, :] for j in range(2)], i == 0, False)
                    if i == 1 and before:
                        layer2_q(g, r - 1)
                    if i == 3 and before:
                        layer2_sum(g, r - 1)
                    matmuls_parts(g, r, i)

            pe.wait_ge(s_w, 16 * NLOADS)
            pe.wait_ge(s_fold, 10)
            layer0(0, 0)
            stages(pe, stage)

            def tower2(n, i, ks=range(U1 // P)):
                lo, hi = TB[n]
                for k in ks:
                    if i == 0:
                        pe.wait_ge(s_m1e, U1 // P * n + k + 1)
                    last = pe.matmul(bank2(i)[:, lo:hi], wt2_sb[:, k, P * i:P * i + P], hid1[:, k, lo:hi],
                                     start=(k == 0), stop=(k == U1 // P - 1))
                if k == U1 // P - 1:
                    last.then_inc(s_m2, 1)

            def tower3(n):
                pe.wait_ge(s_m2e, U2 // P * (n + 1))
                for t in range(TB[n][0] // P, TB[n][1] // P):
                    for k in range(U2 // P):
                        last = pe.matmul(s_ps[:, t:t + 1], hid2[:, k, P * t:P * t + P], wt3_sb[:, k:k + 1],
                                         start=(k == 0), stop=(k == U2 // P - 1))
                return last

            tower2(0, 0, range(0, 3))
            layer2_q(NG - 1, KC - 1)
            tower2(0, 0, range(3, 4))
            tower2(0, 1, range(0, 1))
            layer2_sum(NG - 1, KC - 1)
            tower2(0, 1, range(1, 4))
            for i in range(U1 // P):
                tower1(1, i)
            pe.wait_ge(s_z2, NCH)
            tower3(0)
            for i in range(U2 // P):
                tower2(1, i)
            tower3(1).then_inc(s_y, 1)


def kernel(**inputs):
    import numpy as np
    import concourse.bacc as bacc
    from concourse.bass_utils import run_bass_kernel_spmd

    a = {k: np.asarray(v) for k, v in inputs.items()}
    l = np.arange(F)
    q = np.arange(G4)[:, None]
    w0 = a["L0_rec_W0"].reshape(O, F, F)
    m = (l + q + G4 * np.arange(NS)[:, None, None]) % F
    mo = m[:SLO].transpose(1, 2, 0)
    ll = np.broadcast_to(l[None, :, None], mo.shape)
    w0a = w0[:, ll, mo].transpose(1, 2, 3, 0).reshape(P, SLO, O)
    w0b = w0[:, mo, ll].transpose(1, 2, 3, 0).reshape(P, SLO, O)
    w16 = np.stack([w0[:, l, (l + F // 2) % F].T, w0[:, (l + F // 2) % F, l].T], axis=1)
    w1 = a["L0_rec_W1"].reshape(O, H, F)
    order = np.r_[H:O, 0:H]
    mm = np.broadcast_to(m.transpose(1, 2, 0)[..., None], (G4, F, NS, 2))
    hh = F * ((q[:, :, None, None] + np.arange(2)) % 2) + l[None, :, None, None]
    w1t = w1[order][:, np.broadcast_to(hh, mm.shape), mm].transpose(1, 2, 4, 3, 0).reshape(P, 2, NS, O)
    wt1 = a["W_top1"]
    ids = a["ids"].reshape(P, NT, F).transpose(1, 0, 2).reshape(NCH, 4, NBQ, F)
    ids = ids.transpose(3, 1, 0, 2).reshape(P, NCH, NBQ)
    tables = [a[f"tbl_{f}"] for f in range(F)]
    first_row = np.cumsum([0] + [t.shape[0] for t in tables[:-1]]).astype(np.int32)
    arrays = {
        "ids": ids,
        "first_row": np.repeat(first_row, P // F)[:, None],
        "dense_t": a["dense_ctx"].reshape(P, NT, NDENSE).transpose(2, 1, 0).reshape(NDENSE, B),
        "w0a": w0a, "w0b": w0b, "w16": np.tile(w16, (G4, 1, 1)), "w1": w1t,
        "w2": a["L0_rec_W2"].reshape(H, F),
        "bias_cin": np.stack([a["L0_rec_b0"], a["L0_rec_b1"][order]], axis=1),
        "b2": np.repeat(a["L0_rec_b2"].reshape(1, 1), 4, axis=0),
        "wt1a": wt1[order], "wt1b": np.concatenate([np.repeat(wt1[O:O + 1], 4, axis=0), wt1[O + 1:]]),
        "bt1": a["b_top1"].reshape(U1 // P, P).T,
        "wt2": a["W_top2"].reshape(U1 // P, P, U2).transpose(1, 0, 2),
        "bt2": a["b_top2"].reshape(U2 // P, P).T, "wt3": a["W_top3"].reshape(U2 // P, P).T,
        "ones": np.repeat(np.eye(4, dtype=np.float32), F, axis=0),
        "mask": np.repeat(np.eye(4, dtype=np.float32), NBQ, axis=1).reshape(4, 4, NBQ),
        "signs": np.concatenate([np.tile(np.repeat(np.array([[0], [1]], np.float32), F // 2, axis=0), (G4, 1))] +
                                [np.kron(np.eye(G4, dtype=np.float32),
                                         np.repeat(np.array([[-1], [x]], np.float32), F // 2, axis=0))
                                 for x in (1, 0)], axis=1),
    }
    arrays = {"table": np.concatenate(tables), **{k: np.ascontiguousarray(v) for k, v in arrays.items()}}

    nc = bacc.Bacc("TRN2", target_bir_lowering=False, num_devices=1)

    def dram(name, x):
        return nc.dram_tensor(f"in_{name}", x.shape, mybir.dt.from_np(x.dtype), kind="ExternalInput").ap()
    args = [dram(k, v) for k, v in arrays.items()]
    y = nc.dram_tensor("out_y", (B, 1), F32, kind="ExternalOutput").ap()
    build(nc, *args, y)
    feeds = {f"in_{k}": v for k, v in arrays.items()}
    r = run_bass_kernel_spmd(nc, [feeds], core_ids=[0])
    return r.results[0]["out_y"]
```
